# Optimizing a Trainium2 kernel written in Bass

```python
import numpy as np
import jax
import jax.numpy as jnp

def _softmax(x, axis=-1):
    return jax.nn.softmax(x, axis=axis)

def _gelu(x):
    return jax.nn.gelu(x, approximate=True)

def _silu(x):
    return jax.nn.silu(x)

def _sigmoid(x):
    return jax.nn.sigmoid(x)

def _layernorm(x, axis=-1, eps=1e-05):
    m = jnp.mean(x, axis=axis, keepdims=True)
    v = jnp.var(x, axis=axis, keepdims=True)
    return (x - m) / jnp.sqrt(v + eps)

def _scatter_add(tgt, idx, src, axis=0):
    return tgt.at[idx].add(src)

def _segment_sum(src, seg, n):
    return jax.ops.segment_sum(src, seg, n)
kernel_name = 'mk_sandwich_d1_jaxref_r8_7156fe'

def setup_inputs(seed: int=0):
    np.random.seed(seed)
    _w = jnp.asarray

    def _L0_attn_setup():
        import jax, jax.numpy as jnp
        import numpy as np
        N_EMBD = 128
        N_HEAD = 16
        HEAD_SIZE = 64
        LN_EPS = 0.001
        key = jax.random.key(seed)
        ks = jax.random.split(key, 7)
        B, S, D, H, E = (4, 256, N_EMBD, N_HEAD, HEAD_SIZE)
        x = jax.random.normal(ks[0], (B, S, D), dtype=jnp.float32)
        scale = 1.0 / np.sqrt(D)
        Wq = jax.random.normal(ks[1], (H, D, E), dtype=jnp.float32) * scale
        Wk = jax.random.normal(ks[2], (H, D, E), dtype=jnp.float32) * scale
        Wv = jax.random.normal(ks[3], (H, D, E), dtype=jnp.float32) * scale
        Wo = jax.random.normal(ks[4], (H * E, D), dtype=jnp.float32) * scale
        gamma = jnp.ones((D,), dtype=jnp.float32)
        beta = jnp.zeros((D,), dtype=jnp.float32)
        return {'x': x, 'Wq': Wq, 'Wk': Wk, 'Wv': Wv, 'Wo': Wo, 'gamma': gamma, 'beta': beta}
    _L0_attn_in = _L0_attn_setup()

    def _L0_ffn_setup():
        import jax, jax.numpy as jnp
        import numpy as np
        S, B, H, F, E, K = (256, 4, 128, 512, 8, 2)
        key = jax.random.key(seed)
        k1, k2, k3, k4 = jax.random.split(key, 4)
        scale_h = 1.0 / np.sqrt(H)
        scale_f = 1.0 / np.sqrt(F)
        return {'x': jax.random.normal(k1, (S, B, H), dtype=jnp.float32), 'router_w': jax.random.normal(k2, (H, E), dtype=jnp.float32) * scale_h, 'w1': jax.random.normal(k3, (E, H, F), dtype=jnp.float32) * scale_h, 'w2': jax.random.normal(k4, (E, F, H), dtype=jnp.float32) * scale_f}
    _L0_ffn_in = _L0_ffn_setup()
    _d = {'L0_attn_x': _L0_attn_in['x'], 'L0_attn_Wq': _L0_attn_in['Wq'], 'L0_attn_Wk': _L0_attn_in['Wk'], 'L0_attn_Wv': _L0_attn_in['Wv'], 'L0_attn_Wo': _L0_attn_in['Wo'], 'L0_attn_gamma': _L0_attn_in['gamma'], 'L0_attn_beta': _L0_attn_in['beta'], 'L0_ffn_router_w': _L0_ffn_in['router_w'], 'L0_ffn_w1': _L0_ffn_in['w1'], 'L0_ffn_w2': _L0_ffn_in['w2']}
    _x0 = _d['L0_attn_x']
    _d['L0_attn_x'] = jax.random.normal(jax.random.fold_in(jax.random.key(seed), 1), (16, 256, 128), dtype=_x0.dtype)
    del _x0
    return _d

def reference(L0_attn_x, L0_attn_Wq, L0_attn_Wk, L0_attn_Wv, L0_attn_Wo, L0_attn_gamma, L0_attn_beta, L0_ffn_router_w, L0_ffn_w1, L0_ffn_w2):

    def _L0_attn_ref(x, Wq, Wk, Wv, Wo, gamma, beta):
        import jax, jax.numpy as jnp
        import numpy as np
        N_EMBD = 128
        N_HEAD = 16
        HEAD_SIZE = 64
        LN_EPS = 0.001
        B, S, D = x.shape
        H, _, E = Wq.shape
        q = jnp.einsum('bsd,hde->bhse', x, Wq)
        k = jnp.einsum('bsd,hde->bhse', x, Wk)
        v = jnp.einsum('bsd,hde->bhse', x, Wv)
        scores = jnp.einsum('bhse,bhte->bhst', q, k)
        causal = jnp.tril(jnp.ones((S, S), dtype=bool))
        scores = jnp.where(causal, scores / jnp.sqrt(jnp.float32(E)), jnp.float32(-jnp.inf))
        attn = jax.nn.softmax(scores, axis=-1)
        out = jnp.einsum('bhst,bhte->bhse', attn, v)
        heads = out.transpose(0, 2, 1, 3).reshape(B, S, H * E)
        y = x + heads @ Wo
        mu = jnp.mean(y, axis=-1, keepdims=True)
        var = jnp.mean(jnp.square(y - mu), axis=-1, keepdims=True)
        y = (y - mu) * jax.lax.rsqrt(var + LN_EPS) * gamma + beta
        return y

    def _L0_ffn_ref(x, router_w, w1, w2):
        import jax, jax.numpy as jnp
        import numpy as np
        S, B, H, F, E, K = (256, 4, 128, 512, 8, 2)
        s, b, h = x.shape
        xt = x.reshape(-1, h)
        logits = xt @ router_w
        probs = jax.nn.softmax(logits, axis=-1)
        top_p, top_i = jax.lax.top_k(probs, K)
        out = jnp.zeros_like(xt)
        for e in range(E):
            gate_e = jnp.sum(jnp.where(top_i == e, top_p, 0.0), axis=-1)
            hidden = jax.nn.gelu(xt @ w1[e], approximate=True)
            out = out + gate_e[:, None] * (hidden @ w2[e])
        return out.reshape(s, b, h)
    x = L0_attn_x
    x = x + _layernorm(_L0_attn_ref(_layernorm(x, axis=-1), L0_attn_Wq, L0_attn_Wk, L0_attn_Wv, L0_attn_Wo, L0_attn_gamma, L0_attn_beta), axis=-1)
    x = x + _layernorm(_L0_ffn_ref(_layernorm(x, axis=-1), L0_ffn_router_w, L0_ffn_w1, L0_ffn_w2), axis=-1)
    return x

_drawn_inputs = setup_inputs


def setup_inputs(seed=0):
    import zlib

    import numpy as np

    out = dict(_drawn_inputs(seed))
    spreads = {'L0_attn_gamma': (1.0, 0.2), 'L0_attn_beta': (0.0, 0.1)}
    factors = {}
    for name, (base, spread) in spreads.items():
        noise = np.random.default_rng([zlib.crc32(name.encode()), seed]).standard_normal(out[name].shape)
        drawn = base * np.exp(spread * noise) if base else spread * noise
        out[name] = jnp.asarray(drawn.astype(out[name].dtype))
    for name, factor in factors.items():
        out[name] = (out[name] * factor).astype(out[name].dtype)
    return out
```

```python
from contextlib import ExitStack

import concourse.bass as bass
from concourse import mybir

ALU = mybir.AluOpType
ACT = mybir.ActivationFunctionType
F32 = mybir.dt.float32
F32R = mybir.dt.float32r
BF16 = mybir.dt.bfloat16
U32 = mybir.dt.uint32
I32 = mybir.dt.int32
AX_X = mybir.AxisListType.X

P = 128
LN_EPS = 1e-5
ATT_EPS = 1e-3
MASKED = -3.0e38


def sandwich_kernel(nc, x, wq, wk, wv, wo, gamma, beta, router_w, w1, w2, out):
    B, S, D = x.shape
    H, _, E = wq.shape
    NE, _, F = w1.shape
    T = S // P
    NP = H // 2
    NF = F // P
    NT = B * T
    GT = 4
    NG = NT // GT
    N = NT * P
    K = 2
    CAP = N + P
    TILES = K * NT + NE
    RING = 8
    REC = D + 4
    C_ID, C_GATE = D, D + 1
    SPARE = NE + TILES - K * NT
    assert (D, E, T, NP, F) == (P, P // 2, 2, 8, 512) and NT % GT == 0 and TILES % RING == 0

    x_tiles = x.rearrange("b (t p) d -> b p t d", p=P)
    sent = nc.dram_tensor("sent_rows", ((NE + 1) * CAP, REC), F32, kind="Internal").ap()
    back = nc.dram_tensor("expert_rows", (K * N + SPARE * P, D), F32, kind="Internal").ap()
    back_groups = back[0:K * N, :].rearrange("(r g k p) d -> r g p k d", r=K, k=GT, p=P)
    out_groups = out.rearrange("b (t p) d -> p (b t) d", p=P).rearrange("p (g k) d -> g p k d", k=GT)

    with ExitStack() as ctx:
        def sb(name, shape, dt=F32):
            return ctx.enter_context(nc.sbuf_tensor(name, shape, dt))

        def bank(name):
            return ctx.enter_context(nc.psum_tensor(name, [P, 512], F32))

        sems = {}

        def sem(name):
            if name not in sems:
                sems[name] = ctx.enter_context(nc.semaphore(name))
            return sems[name]

        wqk_in = sb("wqk_in", [P, 2, H, E])
        wq_in, wk_in = wqk_in[:, 0], wqk_in[:, 1]
        wqT = sb("wqT", [P, NP, P])
        wkT = sb("wkT", [P, NP, P])
        m_f = wqk_in[:].rearrange("p a h e -> p (a h e)").rearrange("p (h d) -> p h d", h=H)
        m_hi = sb("m_hi", [P, H, P], F32R)
        m_lo = sb("m_lo", [P, H, P], F32R)
        wv_in = sb("wv_in", [P, H * E])
        wv_hi = sb("wv_hi", [P, H * E], F32R)
        wv_lo = sb("wv_lo", [P, H * E], F32R)
        wo_sb = sb("wo_sb", [P, NP, D])
        w1_in = sb("w1_in", [P, NE, F])
        w1_hi = sb("w1_hi", [P, NE, F], F32R)
        w1_lo = sb("w1_lo", [P, NE, F], F32R)
        w2_sb = sb("w2_sb", [P, NE, NF, D])
        rw_sb = sb("rw_sb", [P, NE])
        gamma_t = sb("gamma_t", [P, T, D])
        beta_t = sb("beta_t", [P, T, D])
        ident = sb("ident", [P, P])
        ident_bf = sb("ident_bf", [P, P], BF16)
        mask = sb("mask", [P, P], BF16)
        half = sb("half", [P, GT])
        ln_eps = sb("ln_eps", [P, GT])
        att_eps = sb("att_eps", [P, GT])

        x_in = sb("x_in", [P, T, D])
        x_res = sb("x_res", [P, T, D])
        xn = sb("xn", [P, T, D])
        xn_res = sb("xn_res", [P, T, D])
        xt_st = sb("xt_st", [P, S])
        xt = sb("xt", [P, S])
        xt_hi = sb("xt_hi", [P, S], F32R)
        xt_lo = sb("xt_lo", [P, S], F32R)
        yq = sb("yq", [P, 2, S])
        v_sb = sb("v_sb", [P, T, H * E])
        prob = sb("prob", [P, 2, 2, 3 * P])
        nmax = sb("nmax", [P, 2, 4])
        den = sb("den", [P, 2, 4])
        rden = sb("rden", [P, 2, 4])
        pT0 = sb("pT0", [P, 2, S])
        pT1 = sb("pT1", [P, 2, P])
        hT = sb("hT", [P, S])
        x1 = sb("x1", [P, NT, D])
        att = sb("att", [P, T, D])
        z1 = sb("z1", [P, T, D])
        z2 = sb("z2", [P, T, D])
        z3 = sb("z3", [P, T, D])
        stat = {k: sb(f"stat_{k}", [P, GT, 6]) for k in ("x", "a", "z", "f", "o0", "o1")}
        mv = {k: sb(f"mv_{k}", [P, GT, 2]) for k in ("x", "a", "z", "f", "o0", "o1")}
        ve = {k: sb(f"ve_{k}", [P, GT]) for k in ("x", "a", "z", "f", "o0", "o1")}
        rstd = {k: sb(f"rstd_{k}", [P, GT]) for k in ("x", "a", "z", "f", "o0", "o1")}

        xf = sb("xf", [P, T, D])

        rec = [sb(f"rec{r}", [P, T, REC]) for r in range(K)]
        xfT = sb("xfT", [P, S])
        rmax = sb("rmax", [P, T])
        lg = sb("lg", [P, T, NE])
        ex = sb("ex", [P, T, NE])
        rsum = sb("rsum", [P, T])
        rrs = sb("rrs", [P, T])
        pr = sb("pr", [P, T, NE])
        top = sb("top", [P, T, 8])
        topi = sb("topi", [P, T, 8], U32)
        topf = sb("topf", [P, T, 8])
        sel = [sb(f"sel{r}", [P, T, NE]) for r in range(K)]
        sel_bf = sb("sel_bf", [P, T, NE], BF16)
        before = sb("before", [P, 2 * T * NE])
        place = sb("place", [P, T, NE])
        picked = sb("picked", [P, K, T, NE])
        slot_f = sb("slot_f", [P, K, T])
        slot = sb("slot", [P, K, T], I32)
        iota_e = sb("iota_e", [P, T, NE])
        ids = sb("ids", [P, K, T])
        base0 = sb("base0", [P, NE])
        base = sb("base", [P, NE])
        earlier = sb("earlier", [P, P], BF16)
        ones_bf = sb("ones_bf", [P, P], BF16)
        pad_rec = sb("pad_rec", [P, SPARE, REC])
        tile_no = sb("tile_no", [1, TILES])
        ones_row = sb("ones_row", [1, NE])
        cnt_f = sb("cnt_f", [1, NE])
        cnt_i = sb("cnt_i", [1, NE], I32)
        n_tiles = sb("n_tiles", [1, NE])
        ends = sb("ends", [1, NE])
        over, over_n = (prob[0:1, i].rearrange("a h c -> a (h c)")[:, 0:TILES * NE]
                        .rearrange("a (n e) -> a n e", e=NE) for i in range(2))
        tile_e = sb("tile_e", [1, TILES])
        tile_s = sb("tile_s", [1, TILES])
        tile_r = sb("tile_r", [1, TILES])
        expert_of = sb("expert_of", [1, TILES], I32)
        row_of = sb("row_of", [1, TILES], I32)
        pad_row = sb("pad_row", [1, NE], I32)

        got = sb("got", [P, RING, REC])
        gT_hi = sb("gT_hi", [P, 2, P], F32R)
        gT_lo = sb("gT_lo", [P, 2, P], F32R)
        hid = sb("hid", [P, 2, F])
        hidT = sb("hidT", [P, F])
        yo = v_sb[:].rearrange("p t c -> p (t c)")[:, 0:RING * D].rearrange("p (k d) -> p k d", k=RING)

        zz = w1_in[:].rearrange("p e f -> p (e f)").rearrange("p (s r k d) -> p s r k d", s=4, r=K, k=GT)
        y_out = sb("y_out", [P, 2, GT, D])

        S1 = [bank("S1a"), bank("S1b")]
        S0, PT0, PT1, O, M, A = (bank(n) for n in ("S0", "PT0", "PT1", "O", "M", "A"))

        y_mm, y_sb = sem("y_mm"), sem("y_sb")
        s1_mm, s0_mm = sem("s1_mm"), sem("s0_mm")
        mx1, mx0, ex1, ex0 = sem("mx1"), sem("mx0"), sem("ex1"), sem("ex0")
        rc, nrm = sem("rc"), sem("nrm")
        t0_mm, t1_mm = sem("t0_mm"), sem("t1_mm")
        pt0_sb, pt1_sb = sem("pt0_sb"), sem("pt1_sb")
        pv_mm, o_sb = sem("pv_mm"), sem("o_sb")
        got_ld = [sem(f"got_ld{k}") for k in range(RING)]
        back_st = [sem(f"back_st{k}") for k in range(RING)]
        zz_ld = [sem(f"zz_ld{k}") for k in range(4)]
        out_st = [sem(f"out_st{k}") for k in range(2)]
        v_mm, v_done = sem("v_mm"), sem("v_done")

        block = ctx.enter_context(nc.Block())

        LAG = 2

        def over_batches(body):
            def run(eng):
                for b in range(LAG):
                    body(b)
                with eng.Fori(LAG, B - 1) as b:
                    body(b)
                for b in range(B - 1, B + LAG):
                    body(b)
            return run

        def there(b, back=0):
            return not isinstance(b, int) or 0 <= b - back < B

        def at(b, n, size):
            return slice(b * n, b * n + size) if isinstance(b, int) else bass.ds(b * n, size)

        @block.sync
        def _(sp):
            sp.dma_start(x_in[:], x_tiles[0]).then_inc(sem("x_in_ld"), 16)
            sp.dma_start(wq_in, wq.rearrange("h d e -> d h e")).then_inc(sem("wqk_ld"), 16)
            sp.dma_start(wk_in, wk.rearrange("h d e -> d h e")).then_inc(sem("wqk_ld"), 16)
            sp.dma_start(wv_in[:].rearrange("p (h e) -> p h e", h=H),
                         wv.rearrange("h d e -> d h e")).then_inc(sem("wv_ld"), 16)
            sp.dma_start(wo_sb[:], wo.rearrange("(c p) d -> p c d", p=P)).then_inc(sem("wo_ld"), 16)
            for t in range(T):
                sp.dma_start(gamma_t[:, t, :], gamma.rearrange("(a d) -> a d", a=1).broadcast_to([P, D]))\
                    .then_inc(sem("gb_ld"), 16)
                sp.dma_start(beta_t[:, t, :], beta.rearrange("(a d) -> a d", a=1).broadcast_to([P, D]))\
                    .then_inc(sem("gb_ld"), 16)
            sp.dma_start(rw_sb[:], router_w).then_inc(sem("ffn_ld"), 16)
            sp.dma_start(w1_in[:], w1.rearrange("e d f -> d e f")).then_inc(sem("w1_ld"), 16)
            for e in range(NE):
                sp.dma_start(w2_sb[:, e], w2[e].rearrange("(c p) d -> p c d", p=P)).then_inc(sem("ffn_ld"), 16)

            sp.wait_ge(sem("pad_ok"), 1)
            sp.dma_start(sent[NE * CAP:NE * CAP + (SPARE - NE) * P, :].rearrange("(k p) c -> p k c", p=P),
                         pad_rec[:, NE:, :]).then_inc(sem("spare_st"), 16)

            def batch(b):
                if there(b, -1) and there(b):
                    sp.wait_ge(sem("xn_done"), b + 1)
                    sp.dma_start(x_in[:], x_tiles[b + 1]).then_inc(sem("x_in_ld"), 16)
                if there(b, 1):
                    if there(b, 2):
                        sp.wait_ge(sem("x1_done"), b - 1)
                    sp.dma_start(x_res[:], x_tiles[b - 1]).then_inc(sem("x_res_ld"), 16)

            over_batches(batch)(sp)

            sp.wait_ge(sem("pads_known"), 1)
            sp.wait_ge(sem("sent_st"), 16 * K * NT)
            for e in range(NE):
                row = sp.value_load(pad_row[0:1, e:e + 1], min_val=0, max_val=NE * CAP - P)
                sp.dma_start(sent[bass.ds(row, P), :], pad_rec[:, e, :]).then_inc(sem("pad_st"), 16)
            sp.wait_ge(sem("pad_st"), 16 * NE)
            sp.wait_ge(sem("spare_st"), 16)
            sp.wait_ge(sem("table_ok"), 1)

            def load_tiles(it, first):
                for k in range(RING):
                    if not first:
                        sp.wait_ge(back_st[k], 16 * it)
                    row = sp.value_load(row_of[0:1, at(it * RING + k, 1, 1)], min_val=0,
                                        max_val=NE * CAP + (SPARE - NE) * P)
                    sp.dma_start(got[:, k, :], sent[bass.ds(row, P), :]).then_inc(got_ld[k], 16)

            load_tiles(0, True)
            with sp.Fori(1, TILES // RING) as it:
                load_tiles(it, False)

            for k in range(RING):
                sp.wait_ge(back_st[k], 16 * (TILES // RING))
            def load_results(g):
                for r in range(K):
                    sp.dma_start(zz[:, g % 4, r], back_groups[r, g]).then_inc(zz_ld[g % 4], 16)

            for g in range(4):
                load_results(g)
            for g in range(NG):
                sp.wait_ge(sem("y_out_done"), g + 1)
                if g + 4 < NG:
                    load_results(g + 4)
                sp.dma_start(out_groups[g], y_out[:, g % 2]).then_inc(out_st[g % 2], 16)
            for k in range(2):
                sp.wait_ge(out_st[k], 16 * (NG // 2))

        @block.tensor
        def _(pe):
            mm = nc.tensor.matmul

            pe.wait_ge(sem("ident_ok"), 1)
            pe.wait_ge(sem("wqk_ld"), 32)
            for n, (src, banks) in enumerate(((wq_in, (S1[0], S1[1])), (wk_in, (S0, PT0)))):
                for c in range(NP):
                    last = nc.tensor.transpose(banks[c // 4][:, (c % 4) * P:(c % 4 + 1) * P],
                                               src[:, 2 * c:2 * c + 2, :].rearrange("p h e -> p (h e)"), ident[:])
                last.then_inc(sem("wT_mm"), 1)
            pe.wait_ge(sem("wT_sb"), 2)
            for h in range(H):
                r = E * (h % 2)
                last = mm((PT1, O, M, A)[h % 2 * 2 + h // 8][:, (h // 2 % 4) * P:(h // 2 % 4 + 1) * P],
                          wqT[r:r + E, h // 2, :], wkT[r:r + E, h // 2, :], start=True, stop=True)
            last.then_inc(sem("m_mm"), 1)

            def product3(dst, a_hi, a_lo, b_hi, b_lo, start=True):
                mm(dst, a_hi, b_hi, start=start, stop=False, skip_group_check=True)
                mm(dst, a_hi, b_lo, start=False, stop=False, skip_group_check=True)
                return mm(dst, a_lo, b_hi, start=False, stop=True, skip_group_check=True)

            def x_transpose(b):
                pe.wait_ge(sem("xn_done"), b + 1)
                for t in range(T):
                    last = nc.tensor.transpose(M[:, t * P:(t + 1) * P], xn[:, t, :], ident[:])
                last.then_inc(sem("xt_mm"), 1)

            def y_proj(c):
                for k in range(2):
                    h = 2 * c + k
                    last = product3(M[:, k * S:(k + 1) * S], m_hi[:, h, :], m_lo[:, h, :],
                                    xt_hi[:], xt_lo[:], start=(k == 0))
                last.then_inc(y_mm, 1)

            def v_proj(t, half_of_heads):
                cols = slice(half_of_heads * 512, half_of_heads * 512 + 512)
                ts = slice(t * P, (t + 1) * P)
                product3(M[:, :], xt_hi[:, ts], xt_lo[:, ts], wv_hi[:, cols], wv_lo[:, cols]).then_inc(v_mm, 1)

            def scores(c):
                bk = S1[c % 2]
                for k in range(2):
                    mm(bk[:, k * S:(k + 1) * S], yq[:, k, P:S], xt[:], start=(k == 0), stop=False,
                       skip_group_check=True)
                for k in range(2):
                    last = mm(bk[:, k * S + P:(k + 1) * S], ident_bf[:], mask[:], start=False, stop=True,
                              skip_group_check=True)
                last.then_inc(s1_mm, 1)

            def scores0():
                for k in range(2):
                    mm(S0[:, k * P:(k + 1) * P], yq[:, k, 0:P], xt[:, 0:P], start=(k == 0), stop=False,
                       skip_group_check=True)
                for k in range(2):
                    last = mm(S0[:, k * P:(k + 1) * P], ident_bf[:], mask[:], start=False, stop=True,
                              skip_group_check=True)
                last.then_inc(s0_mm, 1)

            def pv(c):
                for t, src, cols in ((0, pT0, slice(0, S)), (1, pT1, slice(P, S))):
                    for k in range(2):
                        h = 2 * c + k
                        last = mm(O[k * E:(k + 1) * E, cols], v_sb[:, t, h * E:(h + 1) * E], src[:, k, :],
                                  start=(t == 0), stop=(t == 1), skip_group_check=True)
                last.then_inc(pv_mm, 1)

            def w_o(c):
                for t in range(T):
                    last = mm(A[:, t * D:(t + 1) * D], hT[:, t * P:(t + 1) * P], wo_sb[:, c, :],
                              start=(c == 0 and t == 0), stop=(c == NP - 1), skip_group_check=True)
                if c == NP - 1:
                    last.then_inc(sem("wo_mm"), 1)

            def p_transpose(par):
                for k in range(2):
                    nc.tensor.transpose(PT0[:, k * S:k * S + P], prob[:, par, k, 0:P], ident[:])
                    last = nc.tensor.transpose(PT0[:, k * S + P:(k + 1) * S], prob[:, par, k, P:2 * P], ident[:])
                last.then_inc(t0_mm, 1)
                for k in range(2):
                    last = nc.tensor.transpose(PT1[:, k * P:(k + 1) * P], prob[:, par, k, 2 * P:3 * P], ident[:])
                last.then_inc(t1_mm, 1)

            pe.wait_ge(sem("m_ok"), 1)
            x_transpose(0)
            pe.wait_ge(sem("xt_split"), 1)
            pe.wait_ge(sem("m_split"), 1)
            y_proj(0)
            pe.wait_ge(sem("wv_ok"), 1)
            pe.wait_ge(y_sb, 1)
            v_proj(0, 0)
            pe.wait_ge(v_done, 1)
            v_proj(1, 0)
            pe.wait_ge(sem("xt_ok"), 1)
            pe.wait_ge(sem("mask_ok"), 1)
            scores(0)
            scores0()
            pe.wait_ge(v_done, 2)
            y_proj(1)
            pe.wait_ge(sem("wo_ld"), 16)

            def batch(b):
                for j in range(NP):
                    p = NP * b + j
                    first = isinstance(b, int) and b == 0
                    nxt = there(b) if j < NP - 1 else there(b, -1)
                    nxt2 = there(b) if j < NP - 2 else there(b, -1)
                    last1 = there(b, 1) if j < 1 else there(b)
                    last2 = there(b, 1) if j < 2 else there(b)
                    if nxt and there(b):
                        pe.wait_ge(y_sb, p + 2)
                        if j == NP - 1:
                            pe.wait_ge(sem("xt_ok"), b + 2)
                        if not (first and j == 0):
                            pe.wait_ge(ex1, p)
                        scores((j + 1) % 2)
                        pe.wait_ge(ex0, p + 1)
                        scores0()
                    if last2:
                        pe.wait_ge(o_sb, p - 1)
                        if j == 2 and not first:
                            pe.wait_ge(sem("att_done"), b)
                        w_o((j - 2) % NP)
                    if nxt2 and there(b):
                        if j in (0, 1, 2, 7) and not (first and j == 0):
                            pe.wait_ge(v_done, 4 * b + (5 if j == 7 else j + 2))
                        if j == 5 and there(b, -1):
                            pe.wait_ge(sem("xt_st"), b + 2)
                        if j == 6:
                            pe.wait_ge(sem("xt_split"), b + 2)
                        if there(b, 2):
                            if j == 3:
                                pe.wait_ge(sem("xfT_sb"), b - 1)
                            if j == 4:
                                pe.wait_ge(sem("lg_done"), b - 1)
                        y_proj((j + 2) % NP)
                    if last1:
                        pe.wait_ge(pt0_sb, p)
                        pe.wait_ge(pt1_sb, p)
                        if not (first and j == 1):
                            pe.wait_ge(o_sb, p - 1)
                        if j == 1:
                            pe.wait_ge(v_done, 4 * b + 2)
                        if j == 5:
                            pe.wait_ge(v_done, 4 * b + 4)
                        pv((j - 1) % NP)
                    extra = there(b) and (j in (0, 1) or (j in (4, 6, 7) and there(b, -1)))
                    router = there(b, 2) and j in (2, 3)
                    if (extra or router) and nxt2 and there(b):
                        pe.wait_ge(y_sb, p + 3)
                    if extra:
                        if j in (0, 1):
                            v_proj(j, 1)
                        elif j == 4:
                            x_transpose(b + 1)
                        else:
                            v_proj(j - 6, 0)
                    if router and j == 2:
                        pe.wait_ge(sem("xf_done"), b - 1)
                        for t in range(T):
                            last = nc.tensor.transpose(M[:, t * P:(t + 1) * P], xf[:, t, :], ident[:])
                        last.then_inc(sem("xfT_mm"), 1)
                    if router and j == 3:
                        pe.wait_ge(sem("xfT_sb"), b - 1)
                        for t in range(T):
                            last = mm(M[:, t * NE:(t + 1) * NE], xfT[:, t * P:(t + 1) * P], rw_sb[:],
                                      start=(t == 0), stop=True, skip_group_check=True)
                        last.then_inc(sem("logit_mm"), 1)
                    if there(b):
                        pe.wait_ge(nrm, p + 1)
                        if not (first and j == 0):
                            pe.wait_ge(pt0_sb, p)
                            pe.wait_ge(pt1_sb, p)
                    if there(b, 2) and j == 6:
                        if not there(b):
                            pe.wait_ge(pt1_sb, NP * B)
                            pe.wait_ge(sem("before_sb"), b - 2)
                        rows_before(b - 2)
                    if there(b):
                        p_transpose(j % 2)

            def rows_before(r):
                pe.wait_ge(sem("sel_ok"), r + 1)
                c = 2 * P
                groups = [(0, [(earlier, 0)]), (1, [(earlier, 1), (ones_bf, 0)]), (2, [(ones_bf, 0), (ones_bf, 1)])]
                for g, terms in groups:
                    for n, (lhs, t) in enumerate(terms):
                        last = mm(PT1[:, c + g * NE:c + (g + 1) * NE], lhs[:], sel_bf[:, t, :],
                                  start=(g == 0), stop=(n == len(terms) - 1), skip_group_check=True)
                last.then_inc(sem("before_mm"), 1)

            over_batches(batch)(pe)

            up_bank, out_bank = (S1[0], S1[1]), (O, M)
            w1h = w1_hi[:].rearrange("p e f -> p (e f)")
            w1l = w1_lo[:].rearrange("p e f -> p (e f)")
            w2f = w2_sb[:].rearrange("p e c d -> p (e c d)")
            pe.wait_ge(sem("w1_ok"), 1)
            pe.wait_ge(sem("ffn_ld"), 16 * (NE + 1))
            pe.wait_ge(sem("table_ok"), 1)

            def expert(n):
                return pe.value_load(expert_of[0:1, at(n, 1, 1)], min_val=0, max_val=NE - 1)

            def rows_T(n, k, it, first):
                pe.wait_ge(got_ld[k], 16 * (it + 1))
                if not first:
                    pe.wait_ge(sem("g_split"), n)
                nc.tensor.transpose(PT1[:, 0:P], got[:, k, 0:D], ident[:]).then_inc(sem("gT_mm"), 1)

            def up(n, k, e, first):
                pe.wait_ge(sem("g_split"), n + 1)
                if not first:
                    pe.wait_ge(sem("gelu"), n - 1)
                c = bass.ds(e * F, F)
                product3(up_bank[k % 2][:, :], gT_hi[:, k % 2, :], gT_lo[:, k % 2, :], w1h[:, c], w1l[:, c])\
                    .then_inc(sem("up_mm"), 1)

            def hidden_T(n, k, first):
                pe.wait_ge(sem("gelu"), n + 1)
                if not first:
                    pe.wait_ge(sem("hidT_sb"), n)
                for c in range(NF):
                    last = nc.tensor.transpose(PT0[:, c * P:(c + 1) * P], hid[:, k % 2, c * P:(c + 1) * P], ident[:])
                last.then_inc(sem("hidT_mm"), 1)

            def down(n, k, e, first):
                pe.wait_ge(sem("hidT_sb"), n + 1)
                if not first:
                    pe.wait_ge(sem("yo_done"), n - 1)
                for c in range(NF):
                    last = mm(out_bank[k % 2][:, 0:D], hidT[:, c * P:(c + 1) * P],
                              w2f[:, bass.ds(e * (NF * D) + c * D, D)], start=(c == 0), stop=(c == NF - 1))
                last.then_inc(sem("out_mm"), 1)

            rows_T(0, 0, 0, True)
            rows_T(1, 1, 0, False)
            up(0, 0, expert(0), True)

            def ring(it, first, last):
                e = expert(it * RING)
                for k in range(RING):
                    n = it * RING + k
                    e_next = expert(n + 1) if not (last and k == RING - 1) else None
                    hidden_T(n, k, first and k == 0)
                    if not (last and k >= RING - 2):
                        rows_T(n + 2, (k + 2) % RING, it + (k + 2) // RING, False)
                    if not (last and k == RING - 1):
                        up(n + 1, (k + 1) % RING, e_next, first and k == 0)
                    down(n, k, e, first and k < 2)
                    e = e_next

            ring(0, True, False)
            with pe.Fori(1, TILES // RING - 1) as it:
                ring(it, False, False)
            ring(TILES // RING - 1, False, True)

        @block.vector
        def _(dve):
            v = nc.vector

            def stats(kind, src, tiles, done):
                for t in range(tiles):
                    last = v.bn_stats(stat[kind][:, t, :], src[:, t, :])
                return last

            def moments(kind, tiles):
                for t in range(tiles):
                    last = v.bn_aggr(mv[kind][:, t, :], stat[kind][:, t, :])
                return last

            def normalise(kind, dst, src, tiles):
                for t in range(tiles):
                    last = v.tensor_scalar(dst[:, t, :], src[:, t, :], mv[kind][:, t, 0:1], rstd[kind][:, t:t + 1],
                                           ALU.subtract, ALU.mult)
                return last

            def layer_stats(kind, src, tiles, n):
                stats(kind, src, tiles, n)
                dve.drain()
                moments(kind, tiles).then_inc(sem(f"mv_{kind}"), 1)

            dve.wait_ge(sem("x_in_ld"), 16)
            layer_stats("x", x_in, T, 1)
            dve.wait_ge(sem("wT_mm"), 2)
            v.tensor_copy(wkT[:, 0:4, :], S0[:].rearrange("p (c d) -> p c d", c=4))
            v.tensor_copy(wkT[:, 4:8, :], PT0[:].rearrange("p (c d) -> p c d", c=4)).then_inc(sem("wT_sb"), 1)
            dve.wait_ge(sem("rstd_x"), 1)
            normalise("x", xn, x_in, T).then_inc(sem("xn_done"), 1)
            dve.wait_ge(sem("m_mm"), 1)
            for n, bk in enumerate((PT1, O, M, A)):
                last = v.tensor_scalar(m_f[:, 8 * (n % 2) + n // 2:8 * (n % 2) + 8:2, :], bk[:].rearrange("p (c d) -> p c d", c=4),
                                       float(E) ** -0.5, None, ALU.mult)
            last.then_inc(sem("m_ok"), 1)
            dve.wait_ge(sem("m_ok"), 1)
            v.tensor_copy(m_hi[:], m_f).then_inc(sem("w_hi"), 1)
            dve.wait_ge(sem("w_hi"), 1)
            v.tensor_tensor(m_lo[:], m_f, m_hi[:].bitcast(F32), ALU.subtract).then_inc(sem("m_split"), 1)
            dve.wait_ge(sem("wv_ld"), 16)
            v.tensor_copy(wv_hi[:], wv_in[:]).then_inc(sem("w_hi"), 1)
            dve.wait_ge(sem("w_hi"), 2)
            v.tensor_tensor(wv_lo[:], wv_in[:], wv_hi[:].bitcast(F32), ALU.subtract).then_inc(sem("wv_ok"), 1)

            def x_split(b):
                dve.wait_ge(sem("xt_st"), b + 1)
                v.tensor_copy(xt_hi[:], xt_st[:]).then_inc(sem("xt_h"), 1)
                dve.wait_ge(sem("xt_h"), b + 1)
                v.tensor_tensor(xt_lo[:], xt_st[:], xt_hi[:].bitcast(F32), ALU.subtract).then_inc(sem("xt_split"), 1)

            def maxima(p, par):
                dve.wait_ge(s1_mm, p + 1)
                v.tensor_reduce(nmax[:, par, 0:2], S1[par][:].rearrange("p (k t) -> p k t", k=2), AX_X, ALU.max,
                                negate=True).then_inc(mx1, 1)
                dve.wait_ge(s0_mm, p + 1)
                v.tensor_reduce(nmax[:, par, 2:4], S0[:, 0:2 * P].rearrange("p (k t) -> p k t", k=2), AX_X, ALU.max,
                                negate=True).then_inc(mx0, 1)

            x_split(0)
            dve.wait_ge(sem("xt_split"), 1)
            v.tensor_copy(xt[:], xt_st[:]).then_inc(sem("xt_ok"), 1)
            maxima(0, 0)

            def batch(b):
                for j in range(NP):
                    p = NP * b + j
                    par = j % 2
                    if there(b):
                        dve.wait_ge(ex0, p + 1)
                        v.reciprocal(rden[:, par, :], den[:, par, :]).then_inc(rc, 1)
                        dve.wait_ge(rc, p + 1)
                        for k in range(2):
                            v.tensor_scalar(prob[:, par, k, P:3 * P], prob[:, par, k, P:3 * P],
                                            rden[:, par, k:k + 1], None, ALU.mult)
                            q = v.tensor_scalar(prob[:, par, k, 0:P], prob[:, par, k, 0:P],
                                                rden[:, par, 2 + k:3 + k], None, ALU.mult)
                        q.then_inc(nrm, 1)
                        if j < NP - 1 or there(b, -1):
                            maxima(p + 1, (j + 1) % 2)
                    if there(b, 1):
                        tail(b - 1, j)
                    if there(b) and there(b, -1):
                        ahead(b + 1, j)
                    if there(b, 2):
                        router(b - 2, j)
                    if there(b, 2) and j == NP - 1:
                        dispatch(b - 2)
                    if there(b, 2) and j == 6:
                        if there(b):
                            dve.wait_ge(t1_mm, p + 1)
                        dve.wait_ge(sem("before_mm"), b - 1)
                        v.tensor_copy(before[:, 0:(T + 1) * NE], PT1[:, 2 * P:2 * P + (T + 1) * NE])\
                            .then_inc(sem("before_sb"), 1)
                    if there(b):
                        dve.wait_ge(t1_mm, p + 1)
                        v.tensor_copy(pT1[:], PT1[:, 0:2 * P].rearrange("p (k s) -> p k s", k=2)).then_inc(pt1_sb, 1)

            def over_e(a):
                return a.unsqueeze(2).broadcast_to([P, T, NE])

            def router(r, j):
                if j == 0:
                    rows = x1[:, at(r, T, T), :]
                    dve.wait_ge(sem("x1_done"), r + 1)
                    for t in range(T):
                        v.bn_stats(stat["f"][:, t, :], rows[:, t, :])
                    dve.drain()
                    moments("f", T).then_inc(sem("mv_f"), 1)
                if j == 1:
                    rows = x1[:, at(r, T, T), :]
                    dve.wait_ge(sem("rstd_f"), r + 1)
                    for t in range(T):
                        q = v.tensor_scalar(xf[:, t, :], rows[:, t, :], mv["f"][:, t, 0:1],
                                            rstd["f"][:, t:t + 1], ALU.subtract, ALU.mult)
                    q.then_inc(sem("xf_done"), 1)
                if j == 3:
                    logits = M[:, 0:T * NE].rearrange("p (t e) -> p t e", t=T)
                    dve.wait_ge(sem("logit_mm"), r + 1)
                    v.tensor_reduce(rmax[:], logits, AX_X, ALU.max)
                    dve.drain()
                    v.tensor_tensor(lg[:], logits, over_e(rmax[:]), ALU.subtract).then_inc(sem("lg_done"), 1)
                if j == 4:
                    dve.wait_ge(sem("rexp"), r + 1)
                    v.tensor_reduce(rsum[:], ex[:], AX_X, ALU.add)
                    dve.drain()
                    v.reciprocal(rrs[:], rsum[:])
                    dve.drain()
                    v.tensor_tensor(pr[:], ex[:], over_e(rrs[:]), ALU.mult)
                    dve.drain()
                    for t in range(T):
                        v.max(top[:, t, :], pr[:, t, :])
                    dve.drain()
                    for t in range(T):
                        v.max_index(topi[:, t, :], top[:, t, :], pr[:, t, :])
                    if not (isinstance(r, int) and r == 0):
                        dve.wait_ge(sem("sent_st"), 16 * K * T * r)
                    for k in range(K):
                        v.tensor_copy(rec[k][:, :, C_GATE], top[:, :, k])
                        v.tensor_copy(rec[k][:, :, C_ID].bitcast(I32), ids[:, k, :])
                if j == 5:
                    dve.drain()
                    v.tensor_copy(topf[:], topi[:])
                    v.tensor_scalar(ids[:], ids[:], float(S), None, ALU.add)
                    dve.drain()
                    for k in range(K):
                        v.tensor_tensor(sel[k][:], iota_e[:], over_e(topf[:, :, k]), ALU.is_equal)
                    dve.drain()
                    v.tensor_tensor(sel_bf[:], sel[0][:], sel[1][:], ALU.add).then_inc(sem("sel_ok"), 1)

            def dispatch(r):
                dve.drain()
                v.tensor_tensor(place[:], before[:, 0:T * NE].rearrange("p (t e) -> p t e", t=T),
                                base[:].unsqueeze(1).broadcast_to([P, T, NE]), ALU.add)
                dve.drain()
                v.tensor_tensor(base[:], base[:], before[:, T * NE:(T + 1) * NE], ALU.add)
                for k in range(K):
                    v.tensor_tensor(picked[:, k], place[:], sel[k][:], ALU.mult)
                dve.drain()
                v.tensor_reduce(slot_f[:], picked[:], AX_X, ALU.add)
                dve.drain()
                v.tensor_copy(slot[:], slot_f[:]).then_inc(sem("slot_ok"), 1)

            def ahead(b, j):
                if j == 0:
                    dve.wait_ge(sem("x_in_ld"), 16 * b + 16)
                    layer_stats("x", x_in, T, b + 1)
                if j == 3:
                    dve.wait_ge(sem("rstd_x"), b + 1)
                    dve.wait_ge(sem("xn_kept"), b)
                    normalise("x", xn, x_in, T).then_inc(sem("xn_done"), 1)
                if j == 5:
                    dve.wait_ge(y_mm, NP * b)
                    x_split(b)
                if j == 6:
                    v.tensor_copy(xt[:], xt_st[:]).then_inc(sem("xt_ok"), 1)

            def tail(b, j):
                if j == 1:
                    dve.wait_ge(sem("wo_mm"), b + 1)
                    v.tensor_tensor(att[:], xn_res[:], A[:, 0:T * D].rearrange("p (t d) -> p t d", t=T), ALU.add)\
                        .then_inc(sem("att_done"), 1)
                    dve.wait_ge(sem("att_done"), b + 1)
                    layer_stats("a", att, T, b + 1)
                if j == 2:
                    dve.wait_ge(sem("rstd_a"), b + 1)
                    normalise("a", z1, att, T).then_inc(sem("z1_done"), 1)
                if j == 4:
                    dve.wait_ge(sem("z2_done"), b + 1)
                    layer_stats("z", z2, T, b + 1)
                if j == 6:
                    dve.wait_ge(sem("rstd_z"), b + 1)
                    normalise("z", z3, z2, T).then_inc(sem("z3_done"), 1)

            dve.wait_ge(sem("consts_ok"), 1)
            v.tensor_copy(base[:], base0[:])
            over_batches(batch)(dve)

            def over_tiles(a):
                return a.unsqueeze(1).broadcast_to([1, TILES, NE])

            dve.drain()
            v.tensor_copy(pad_row[:], base[0:1, :]).then_inc(sem("pads_known"), 1)
            v.tensor_tensor(cnt_f[:], base[0:1, :], base0[0:1, :], ALU.subtract)
            dve.drain()
            v.tensor_scalar(cnt_i[:], cnt_f[:], float(P - 1), None, ALU.add)
            dve.drain()
            v.tensor_scalar(cnt_i[:], cnt_i[:], P.bit_length() - 1, None, ALU.logical_shift_right)
            dve.drain()
            v.tensor_copy(n_tiles[:], cnt_i[:])
            dve.drain()
            v.tensor_tensor_scan(ends[:], ones_row[:], n_tiles[:], 0.0, ALU.mult, ALU.add)
            dve.drain()
            v.tensor_tensor(over, over_tiles(ends[:]), tile_no[:].unsqueeze(2).broadcast_to([1, TILES, NE]),
                            ALU.is_le)
            dve.drain()
            v.tensor_reduce(tile_e[:], over, AX_X, ALU.add)
            v.tensor_tensor(over_n, over, over_tiles(n_tiles[:]), ALU.mult)
            dve.drain()
            v.tensor_reduce(tile_s[:], over_n, AX_X, ALU.add)
            v.tensor_scalar(expert_of[:], tile_e[:], float(NE - 1), None, ALU.min)
            dve.drain()
            v.tensor_tensor(tile_s[:], tile_no[:], tile_s[:], ALU.subtract)
            v.tensor_scalar(tile_e[:], tile_e[:], float(CAP), None, ALU.mult)
            dve.drain()
            v.tensor_scalar(tile_s[:], tile_s[:], float(P), None, ALU.mult)
            dve.drain()
            v.tensor_tensor(tile_r[:], tile_s[:], tile_e[:], ALU.add)
            dve.drain()
            v.tensor_copy(row_of[:], tile_r[:]).then_inc(sem("table_ok"), 1)

            def split_rows(n, k):
                dve.wait_ge(sem("gT_mm"), n + 1)
                v.tensor_copy(gT_hi[:, k % 2, :], PT1[:, 0:P]).then_inc(sem("g_h"), 1)
                dve.wait_ge(sem("g_h"), n + 1)
                v.tensor_tensor(gT_lo[:, k % 2, :], PT1[:, 0:P], gT_hi[:, k % 2, :].bitcast(F32), ALU.subtract)\
                    .then_inc(sem("g_split"), 1)

            split_rows(0, 0)
            split_rows(1, 1)

            def ring(n0, last):
                for k in range(RING):
                    dve.wait_ge(sem("hidT_mm"), n0 + k + 1)
                    v.tensor_copy(hidT[:], PT0[:]).then_inc(sem("hidT_sb"), 1)
                    if not (last and k >= RING - 2):
                        if isinstance(n0, int) and n0 == 0 and k == 0:
                            dve.wait_ge(sem("up_mm"), 1)
                        split_rows(n0 + k + 2, k)

            ring(0, False)
            with dve.Fori(1, TILES // RING - 1) as it:
                ring(it * RING, False)
            ring(TILES - RING, True)

            for g in range(NG + 1):
                if g < NG:
                    z = zz[:, g % 4]
                    o = f"o{g % 2}"
                    dve.wait_ge(zz_ld[g % 4], 16 * K * (g // 4 + 1))
                    v.tensor_tensor(z[:, 0], z[:, 0], z[:, 1], ALU.add)
                    dve.drain()
                    for t in range(GT):
                        v.bn_stats(stat[o][:, t, :], z[:, 0, t, :])
                    dve.drain()
                    if g >= 2:
                        dve.wait_ge(sem("zn_done"), g - 1)
                    for t in range(GT):
                        q = v.bn_aggr(mv[o][:, t, :], stat[o][:, t, :])
                    q.then_inc(sem("mv_o"), 1)
                if g >= 1:
                    h = g - 1
                    z = zz[:, h % 4]
                    o = f"o{h % 2}"
                    dve.wait_ge(sem("rstd_o"), h + 1)
                    for t in range(GT):
                        q = v.tensor_scalar(z[:, 0, t, :], z[:, 0, t, :], mv[o][:, t, 0:1], rstd[o][:, t:t + 1],
                                            ALU.subtract, ALU.mult)
                    q.then_inc(sem("zn_done"), 1)

        @block.scalar
        def _(act):
            a = nc.scalar
            act.wait_ge(sem("wT_mm"), 1)
            a.activation(wqT[:, 0:4, :], S1[0][:].rearrange("p (c d) -> p c d", c=4), ACT.Copy)
            a.activation(wqT[:, 4:8, :], S1[1][:].rearrange("p (c d) -> p c d", c=4), ACT.Copy)\
                .then_inc(sem("wT_sb"), 1)

            def xt_copy(b):
                act.wait_ge(sem("xt_mm"), b + 1)
                a.activation(xt_st[:], M[:, 0:S], ACT.Copy).then_inc(sem("xt_st"), 1)

            def y_copy(p):
                act.wait_ge(y_mm, p + 1)
                a.activation(yq[:], M[:].rearrange("p (k s) -> p k s", k=2), ACT.Copy).then_inc(y_sb, 1)

            def exps(p, par):
                act.wait_ge(mx1, p + 1)
                for k in range(2):
                    q = a.activation(prob[:, par, k, P:3 * P], S1[par][:, k * S:(k + 1) * S], ACT.Exp,
                                     bias=nmax[:, par, k:k + 1], accum_out=den[:, par, k:k + 1])
                q.then_inc(ex1, 1)
                act.wait_ge(mx0, p + 1)
                for k in range(2):
                    q = a.activation(prob[:, par, k, 0:P], S0[:, k * P:(k + 1) * P], ACT.Exp,
                                     bias=nmax[:, par, 2 + k:3 + k], accum_out=den[:, par, 2 + k:3 + k])
                q.then_inc(ex0, 1)

            def v_copy(n, t, half_of_heads):
                act.wait_ge(v_mm, n)
                a.activation(v_sb[:, t, half_of_heads * 512:half_of_heads * 512 + 512], M[:], ACT.Copy)\
                    .then_inc(v_done, 1)

            def o_copy(p):
                act.wait_ge(pv_mm, p + 1)
                a.activation(hT[:], O[:, 0:S], ACT.Copy).then_inc(o_sb, 1)

            xt_copy(0)
            y_copy(0)
            v_copy(1, 0, 0)
            v_copy(2, 1, 0)
            act.wait_ge(s0_mm, 1)
            y_copy(1)
            exps(0, 0)

            def batch(b):
                for j in range(NP):
                    p = NP * b + j
                    first = isinstance(b, int) and b == 0
                    if there(b):
                        if j < NP - 2 or there(b, -1):
                            y_copy(p + 2)
                        if j < NP - 1 or there(b, -1):
                            if not (first and j == 0):
                                act.wait_ge(t1_mm, p)
                            exps(p + 1, (j + 1) % 2)
                    if (there(b) and not (first and j == 0)) or (j == 0 and there(b, 1)):
                        o_copy(p - 1)
                    if there(b):
                        if there(b, -1) and j == 4:
                            act.wait_ge(sem("xt_ok"), b + 1)
                            xt_copy(b + 1)
                        if j in (0, 1):
                            v_copy(4 * b + 3 + j, j, 1)
                        if there(b, -1) and j in (6, 7):
                            v_copy(4 * b + j - 1, j - 6, 0)
                    if there(b, 2):
                        if j == 2:
                            act.wait_ge(sem("xfT_mm"), b - 1)
                            a.activation(xfT[:], M[:, 0:S], ACT.Copy).then_inc(sem("xfT_sb"), 1)
                        if j == 3:
                            act.wait_ge(sem("lg_done"), b - 1)
                            a.activation(ex[:], lg[:], ACT.Exp).then_inc(sem("rexp"), 1)
                        if j == 5:
                            if there(b, 3):
                                act.wait_ge(sem("sent_st"), 16 * K * T * (b - 2))
                            for k in range(K):
                                q = a.activation(rec[k][:, :, 0:D], xf[:], ACT.Copy)
                            q.then_inc(sem("rec_ok"), 1)
                    if there(b):
                        act.wait_ge(t0_mm, p + 1)
                        a.activation(pT0[:], PT0[:].rearrange("p (k s) -> p k s", k=2), ACT.Copy)\
                            .then_inc(pt0_sb, 1)

            over_batches(batch)(act)

            def gelu(n, k, first):
                act.wait_ge(sem("up_mm"), n + 1)
                if not first:
                    act.wait_ge(sem("hidT_mm"), n - 1)
                a.activation(hid[:, k % 2, :], S1[k % 2][:], ACT.Gelu_apprx_tanh).then_inc(sem("gelu"), 1)

            def ring(it, first, last):
                for k in range(RING):
                    n = it * RING + k
                    if not (last and k == RING - 1):
                        gelu(n + 1, (k + 1) % RING, first and k == 0)
                    act.wait_ge(sem("out_mm"), n + 1)
                    if not first:
                        act.wait_ge(back_st[k], 16 * it)
                    a.activation(yo[:, k, :], (O, M)[k % 2][:, 0:D], ACT.Copy, scale=got[:, k, C_GATE:C_GATE + 1])\
                        .then_inc(sem("yo_done"), 1)

            gelu(0, 0, True)
            ring(0, True, False)
            with act.Fori(1, TILES // RING - 1) as it:
                ring(it, False, False)
            ring(TILES // RING - 1, False, True)

        @block.gpsimd
        def _(pool):
            q = nc.gpsimd
            q.memset(ident[:], 0.0)
            q.memset(half[:], -0.5)
            q.memset(ln_eps[:], LN_EPS)
            q.memset(att_eps[:], ATT_EPS)
            q.memset(mask[:], 0.0).then_inc(sem("p_set"), 1)
            pool.wait_ge(sem("p_set"), 1)
            q.affine_select(out=ident[:], in_=ident[:], compare_op=ALU.not_equal, fill=1.0, base=0,
                            pattern=[[-1, P]], channel_multiplier=1).then_inc(sem("ident_ok"), 1)
            pool.wait_ge(sem("ident_ok"), 1)
            q.tensor_copy(ident_bf[:], ident[:])
            q.affine_select(out=mask[:], in_=mask[:], compare_op=ALU.is_ge, fill=MASKED, base=0,
                            pattern=[[-1, P]], channel_multiplier=1).then_inc(sem("mask_ok"), 1)
            q.memset(ones_bf[:], 1.0)
            q.memset(earlier[:], 1.0)
            q.memset(ones_row[:], 1.0)
            q.memset(pad_rec[:], 0.0)
            for r in rec:
                q.memset(r[:], 0.0)
            q.iota(iota_e[:], pattern=[[0, T], [1, NE]], base=0, channel_multiplier=0,
                   allow_small_or_imprecise_dtypes=True)
            q.iota(ids[:], pattern=[[N, K], [P, T]], base=0, channel_multiplier=1,
                   allow_small_or_imprecise_dtypes=True)
            q.iota(base0[:], pattern=[[CAP, NE]], base=0, channel_multiplier=0,
                   allow_small_or_imprecise_dtypes=True)
            q.iota(tile_no[:], pattern=[[1, TILES]], base=0, channel_multiplier=0,
                   allow_small_or_imprecise_dtypes=True).then_inc(sem("iota_ok"), 1)
            pool.wait_ge(sem("iota_ok"), 1)
            q.affine_select(out=earlier[:], in_=earlier[:], compare_op=ALU.is_gt, fill=0.0, base=0,
                            pattern=[[1, P]], channel_multiplier=-1).then_inc(sem("consts_ok"), 1)
            q.iota(pad_rec[:, :, C_ID].bitcast(I32), pattern=[[P, SPARE]], base=K * N, channel_multiplier=1)\
                .then_inc(sem("pad_ok"), 1)

            def inverse_root(kind, tiles, eps, n):
                pool.wait_ge(sem(f"mv_{kind}"), n)
                q.tensor_tensor(ve[kind][:, 0:tiles], mv[kind][:, 0:tiles, 1], eps[:, 0:tiles], ALU.add)\
                    .then_inc(sem(f"ve_{kind}"), 1)
                pool.wait_ge(sem(f"ve_{kind}"), n)
                q.tensor_tensor(rstd[kind][:, 0:tiles], ve[kind][:, 0:tiles], half[:, 0:tiles], ALU.pow)\
                    .then_inc(sem(f"rstd_{kind}"), 1)

            inverse_root("x", T, ln_eps, 1)
            pool.wait_ge(sem("gb_ld"), 16 * 2 * T)
            pool.wait_ge(sem("xn_done"), 1)
            q.tensor_copy(xn_res[:], xn[:]).then_inc(sem("xn_kept"), 1)
            pool.wait_ge(sem("w1_ld"), 16)
            q.tensor_copy(w1_hi[:], w1_in[:]).then_inc(sem("w1_h"), 1)
            pool.wait_ge(sem("w1_h"), 1)
            q.tensor_tensor(w1_lo[:], w1_in[:], w1_hi[:].bitcast(F32), ALU.subtract).then_inc(sem("w1_ok"), 1)

            def tail(b):
                inverse_root("a", T, att_eps, b + 1)
                if not (isinstance(b, int) and b == B - 1):
                    q.tensor_copy(xn_res[:], xn[:]).then_inc(sem("xn_kept"), 1)
                pool.wait_ge(sem("z1_done"), b + 1)
                q.tensor_tensor(z2[:], z1[:], gamma_t[:], ALU.mult).then_inc(sem("z_g"), 1)
                pool.wait_ge(sem("z_g"), b + 1)
                q.tensor_tensor(z2[:], z2[:], beta_t[:], ALU.add).then_inc(sem("z2_done"), 1)

            def tail_end(b):
                inverse_root("z", T, ln_eps, b + 1)
                pool.wait_ge(sem("z3_done"), b + 1)
                pool.wait_ge(sem("x_res_ld"), 16 * b + 16)
                q.tensor_tensor(x1[:, at(b, T, T), :], x_res[:], z3[:], ALU.add).then_inc(sem("x1_done"), 1)

            def send(r):
                pool.wait_ge(sem("slot_ok"), r + 1)
                pool.wait_ge(sem("rec_ok"), r + 1)
                q.sem_inc(sem("send_turn"), 1)
                for k in range(K):
                    for t in range(T):
                        q.indirect_dma_start(sent, bass.IndirectOffsetOnAxis(ap=slot[:, k, t:t + 1], axis=0),
                                             rec[k][:, t, :], None).then_inc(sem("sent_st"), 16)

            def batch(b):
                if there(b) and there(b, -1):
                    inverse_root("x", T, ln_eps, b + 2)
                if there(b, 2):
                    inverse_root("f", T, ln_eps, b - 1)
                if there(b, 1):
                    tail(b - 1)
                    tail_end(b - 1)
                if there(b, 2):
                    send(b - 2)

            over_batches(batch)(pool)

            def store(n, k):
                pool.wait_ge(sem("yo_done"), n + 1)
                q.sem_inc(sem("store_turn"), 1)
                q.indirect_dma_start(back, bass.IndirectOffsetOnAxis(ap=got[:, k, C_ID:C_ID + 1].bitcast(I32), axis=0),
                                     yo[:, k, :], None).then_inc(back_st[k], 16)

            with pool.Fori(0, TILES // RING) as it:
                for k in range(RING):
                    store(it * RING + k, k)

            for g in range(NG + 1):
                if g < NG:
                    o = f"o{g % 2}"
                    pool.wait_ge(sem("mv_o"), g + 1)
                    q.tensor_tensor(ve[o][:], mv[o][:, :, 1], ln_eps[:], ALU.add).then_inc(sem("ve_o"), 1)
                    pool.wait_ge(sem("ve_o"), g + 1)
                    q.tensor_tensor(rstd[o][:], ve[o][:], half[:], ALU.pow).then_inc(sem("rstd_o"), 1)
                if g >= 1:
                    h = g - 1
                    pool.wait_ge(sem("zn_done"), g)
                    if h >= 2:
                        pool.wait_ge(out_st[h % 2], 16 * (h // 2))
                    q.tensor_tensor(y_out[:, h % 2], x1[:, h * GT:(h + 1) * GT, :], zz[:, h % 4, 0], ALU.add)\
                        .then_inc(sem("y_out_done"), 1)


_INS = ["L0_attn_x", "L0_attn_Wq", "L0_attn_Wk", "L0_attn_Wv", "L0_attn_Wo", "L0_attn_gamma", "L0_attn_beta",
        "L0_ffn_router_w", "L0_ffn_w1", "L0_ffn_w2"]


def kernel(**inputs):
    import numpy as np
    import concourse.bacc as bacc
    from concourse.bass_utils import run_bass_kernel_spmd

    nc = bacc.Bacc("TRN2", target_bir_lowering=False, num_devices=1)
    arrays, args = {}, []
    for name in _INS:
        a = np.ascontiguousarray(inputs[name])
        arrays[name] = a
        args.append(nc.dram_tensor(name, a.shape, mybir.dt.from_np(a.dtype), kind="ExternalInput").ap())
    out = nc.dram_tensor("out", arrays["L0_attn_x"].shape, F32, kind="ExternalOutput").ap()
    sandwich_kernel(nc, *args, out)
    r = run_bass_kernel_spmd(nc, [arrays], core_ids=[0])
    return r.results[0]["out"]
```

```python
from contextlib import ExitStack

import concourse.bass as bass
from concourse import mybir

ALU = mybir.AluOpType
ACT = mybir.ActivationFunctionType
F32 = mybir.dt.float32
F32R = mybir.dt.float32r
BF16 = mybir.dt.bfloat16
U32 = mybir.dt.uint32
I32 = mybir.dt.int32
AX_X = mybir.AxisListType.X

P = 128
LN_EPS = 1e-5
ATT_EPS = 1e-3
MASKED = -3.0e38


def sandwich_kernel(nc, x, wq, wk, wv, wo, gamma, beta, router_w, w1, w2, out):
    B, S, D = x.shape
    H, _, E = wq.shape
    NE, _, F = w1.shape
    T = S // P
    NP = H // 2
    NF = F // P
    NT = B * T
    GT = 4
    NG = NT // GT
    N = NT * P
    K = 2
    CAP = N + P
    TILES = K * NT + NE
    RING = 8
    REC = D + 4
    C_ID, C_GATE = D, D + 1
    SPARE = NE + TILES - K * NT
    assert (D, E, T, NP, F) == (P, P // 2, 2, 8, 512) and NT % GT == 0 and TILES % RING == 0

    x_tiles = x.rearrange("b (t p) d -> b p t d", p=P)
    sent = nc.dram_tensor("sent_rows", ((NE + 1) * CAP, REC), F32, kind="Internal").ap()
    back = nc.dram_tensor("expert_rows", (K * N + SPARE * P, D), F32, kind="Internal").ap()
    back_groups = back[0:K * N, :].rearrange("(r g k p) d -> r g p k d", r=K, k=GT, p=P)
    out_groups = out.rearrange("b (t p) d -> p (b t) d", p=P).rearrange("p (g k) d -> g p k d", k=GT)

    with ExitStack() as ctx:
        def sb(name, shape, dt=F32):
            return ctx.enter_context(nc.sbuf_tensor(name, shape, dt))

        def bank(name):
            return ctx.enter_context(nc.psum_tensor(name, [P, 512], F32))

        sems = {}

        def sem(name):
            if name not in sems:
                sems[name] = ctx.enter_context(nc.semaphore(name))
            return sems[name]

        wqk_in = sb("wqk_in", [P, 2, H, E])
        wq_in, wk_in = wqk_in[:, 0], wqk_in[:, 1]
        wqT = sb("wqT", [P, NP, P])
        wkT = sb("wkT", [P, NP, P])
        m_hi = sb("m_hi", [P, H, P], F32R)
        m_lo = sb("m_lo", [P, H, P], F32R)
        wv_in = sb("wv_in", [P, H * E])
        wv_hi = sb("wv_hi", [P, H * E], F32R)
        wv_lo = sb("wv_lo", [P, H * E], F32R)
        wo_sb = sb("wo_sb", [P, NP, D])
        w1_in = sb("w1_in", [P, NE, F])
        w1_hi = sb("w1_hi", [P, NE, F], F32R)
        w1_lo = sb("w1_lo", [P, NE, F], F32R)
        w2_sb = sb("w2_sb", [P, NE, NF, D])
        rw_sb = sb("rw_sb", [P, NE])
        gamma_t = sb("gamma_t", [P, T, D])
        beta_t = sb("beta_t", [P, T, D])
        ident = sb("ident", [P, P])
        ident_bf = sb("ident_bf", [P, P], BF16)
        mask = sb("mask", [P, P], BF16)
        half = sb("half", [P, GT])
        ln_eps = sb("ln_eps", [P, GT])
        att_eps = sb("att_eps", [P, GT])

        x_in = sb("x_in", [P, T, D])
        x_res = sb("x_res", [P, T, D])
        xn = sb("xn", [P, T, D])
        xn_res = sb("xn_res", [P, T, D])
        xt_st = sb("xt_st", [P, S])
        xt = sb("xt", [P, P])
        xs_hi = sb("xs_hi", [P, S], F32R)
        xs_lo = sb("xs_lo", [P, S], F32R)
        xt_hi = sb("xt_hi", [P, S], F32R)
        xt_lo = sb("xt_lo", [P, S], F32R)
        yq = sb("yq", [P, 2, S])
        yq_hi = sb("yq_hi", [P, 2, P], F32R)
        yq_lo = sb("yq_lo", [P, 2, P], F32R)
        v_sb = sb("v_sb", [P, T, H * E])
        prob = sb("prob", [P, 2, 2, 3 * P])
        nmax = sb("nmax", [P, 2, 4])
        den = sb("den", [P, 2, 4])
        rden = sb("rden", [P, 2, 4])
        pT0 = sb("pT0", [P, 2, S])
        pT1 = sb("pT1", [P, 2, P])
        hT = sb("hT", [P, S])
        zn = sb("zn", [P, 2, GT, D])
        shift = sb("shift", [P, 2, GT])
        x1 = sb("x1", [P, NT, D])
        att = sb("att", [P, T, D])
        z1 = sb("z1", [P, T, D])
        z2 = sb("z2", [P, T, D])
        z3 = sb("z3", [P, T, D])
        stat = {k: sb(f"stat_{k}", [P, GT, 6]) for k in ("x", "a", "z", "f", "o0", "o1")}
        mv = {k: sb(f"mv_{k}", [P, GT, 2]) for k in ("x", "a", "z", "f", "o0", "o1")}
        ve = {k: sb(f"ve_{k}", [P, GT]) for k in ("x", "a", "z", "f", "o0", "o1")}
        rstd = {k: sb(f"rstd_{k}", [P, GT]) for k in ("x", "a", "z", "f", "o0", "o1")}

        xf = sb("xf", [P, T, D])

        rec = [sb(f"rec{r}", [P, T, REC]) for r in range(K)]
        xfT = sb("xfT", [P, S])
        rmax = sb("rmax", [P, T])
        lg = sb("lg", [P, T, NE])
        ex = sb("ex", [P, T, NE])
        rsum = sb("rsum", [P, T])
        rrs = sb("rrs", [P, T])
        pr = sb("pr", [P, T, NE])
        top = sb("top", [P, T, 8])
        topi = sb("topi", [P, T, 8], U32)
        topf = sb("topf", [P, T, 8])
        sel = [sb(f"sel{r}", [P, T, NE]) for r in range(K)]
        sel_bf = sb("sel_bf", [P, T, NE], BF16)
        before = sb("before", [P, 2 * T * NE])
        place = sb("place", [P, T, NE])
        picked = sb("picked", [P, K, T, NE])
        slot_f = sb("slot_f", [P, K, T])
        slot = sb("slot", [P, K, T], I32)
        iota_e = sb("iota_e", [P, T, NE])
        ids = sb("ids", [P, K, T])
        base0 = sb("base0", [P, NE])
        base = sb("base", [P, NE])
        earlier = sb("earlier", [P, P], BF16)
        ones_bf = sb("ones_bf", [P, P], BF16)
        pad_rec = sb("pad_rec", [P, SPARE, REC])
        tile_no = sb("tile_no", [1, TILES])
        ones_row = sb("ones_row", [1, NE])
        cnt_f = sb("cnt_f", [1, NE])
        cnt_i = sb("cnt_i", [1, NE], I32)
        n_tiles = sb("n_tiles", [1, NE])
        ends = sb("ends", [1, NE])
        over, over_n = (prob[0:1, i].rearrange("a h c -> a (h c)")[:, 0:TILES * NE]
                        .rearrange("a (n e) -> a n e", e=NE) for i in range(2))
        tile_e = sb("tile_e", [1, TILES])
        tile_s = sb("tile_s", [1, TILES])
        tile_r = sb("tile_r", [1, TILES])
        expert_of = sb("expert_of", [1, TILES + RING], I32)
        row_of = sb("row_of", [1, TILES], I32)
        pad_row = sb("pad_row", [1, NE], I32)

        got = sb("got", [P, RING, REC])
        gT_hi = sb("gT_hi", [P, 2, P], F32R)
        gT_lo = sb("gT_lo", [P, 2, P], F32R)
        hid = sb("hid", [P, 2, F])
        hidT = sb("hidT", [P, 2, F])
        yo = v_sb[:].rearrange("p t c -> p (t c)")[:, 0:RING * D].rearrange("p (k d) -> p k d", k=RING)

        zz = w1_in[:].rearrange("p e f -> p (e f)").rearrange("p (s r k d) -> p s r k d", s=4, r=K, k=GT)
        y_out = sb("y_out", [P, 2, GT, D])

        S1 = [bank("S1a"), bank("S1b")]
        S0, PT0, PT1, O, M, A = (bank(n) for n in ("S0", "PT0", "PT1", "O", "M", "A"))

        y_mm, y_sb = sem("y_mm"), sem("y_sb")
        s1_mm, s0_mm = sem("s1_mm"), sem("s0_mm")
        mx1, mx0, ex1, ex0 = sem("mx1"), sem("mx0"), sem("ex1"), sem("ex0")
        rc, nrm = sem("rc"), sem("nrm")
        t0_mm, t1_mm = sem("t0_mm"), sem("t1_mm")
        pt0_sb, pt1_sb = sem("pt0_sb"), sem("pt1_sb")
        pv_mm, o_sb = sem("pv_mm"), sem("o_sb")
        got_ld = [sem(f"got_ld{k}") for k in range(RING)]
        back_st = [sem(f"back_st{k}") for k in range(RING)]
        zz_ld = [sem(f"zz_ld{k}") for k in range(4)]
        out_st = [sem(f"out_st{k}") for k in range(2)]
        v_mm, v_done = sem("v_mm"), sem("v_done")
        y_h, y_lo = sem("y_h"), sem("y_lo")

        block = ctx.enter_context(nc.Block())

        sum_bank = (S1[0], S1[1], S0, PT0)

        m_banks = ((PT1, O), (A, PT0))

        def m_part(m, g, i):
            return m[:, 8 * g + i:8 * g + 8:2, :]

        LAG = 2

        def over_batches(body):
            def run(eng):
                for b in range(LAG + 1):
                    body(b)
                with eng.Fori(LAG + 1, B - 1) as b:
                    body(b)
                for b in range(B - 1, B + LAG):
                    body(b)
            return run

        def there(b, back=0):
            return not isinstance(b, int) or 0 <= b - back < B

        def at(b, n, size):
            return slice(b * n, b * n + size) if isinstance(b, int) else bass.ds(b * n, size)

        @block.sync
        def _(sp):
            sp.dma_start(x_in[:], x_tiles[0]).then_inc(sem("x_in_ld"), 16)
            sp.dma_start(wq_in, wq.rearrange("h d e -> d h e")).then_inc(sem("wq_ld"), 16)
            sp.dma_start(wk_in, wk.rearrange("h d e -> d h e")).then_inc(sem("wk_ld"), 16)
            sp.dma_start(wv_in[:].rearrange("p (h e) -> p h e", h=H),
                         wv.rearrange("h d e -> d h e")).then_inc(sem("wv_ld"), 16)
            sp.dma_start(wo_sb[:], wo.rearrange("(c p) d -> p c d", p=P)).then_inc(sem("wo_ld"), 16)
            for t in range(T):
                sp.dma_start(gamma_t[:, t, :], gamma.rearrange("(a d) -> a d", a=1).broadcast_to([P, D]))\
                    .then_inc(sem("gb_ld"), 16)
                sp.dma_start(beta_t[:, t, :], beta.rearrange("(a d) -> a d", a=1).broadcast_to([P, D]))\
                    .then_inc(sem("gb_ld"), 16)
            sp.dma_start(rw_sb[:], router_w).then_inc(sem("ffn_ld"), 16)
            sp.dma_start(w1_in[:], w1.rearrange("e d f -> d e f")).then_inc(sem("w1_ld"), 16)
            for e in range(NE):
                sp.dma_start(w2_sb[:, e], w2[e].rearrange("(c p) d -> p c d", p=P)).then_inc(sem("ffn_ld"), 16)

            sp.wait_ge(sem("pad_ok"), 1)
            sp.dma_start(sent[NE * CAP:NE * CAP + (SPARE - NE) * P, :].rearrange("(k p) c -> p k c", p=P),
                         pad_rec[:, NE:, :]).then_inc(sem("spare_st"), 16)

            def batch(b):
                if there(b, -1) and there(b):
                    sp.wait_ge(sem("xn_done"), b + 1)
                    sp.dma_start(x_in[:], x_tiles[b + 1]).then_inc(sem("x_in_ld"), 16)
                if there(b, 1):
                    if there(b, 2):
                        sp.wait_ge(sem("x1_done"), b - 1)
                    sp.dma_start(x_res[:], x_tiles[b - 1]).then_inc(sem("x_res_ld"), 16)

            over_batches(batch)(sp)

            def table_values(row, largest, why):
                return nc.values_load_multi_w_load_instructions(
                    row, engines=[mybir.EngineType.SP], min_val=0, max_val=largest,
                    skip_runtime_bounds_check_because=why)[1]

            sp.wait_ge(sem("pads_known"), 1)
            rows = table_values(pad_row[0:1, :], NE * CAP - P, "an expert gets N rows at most, its region has CAP")
            for e in range(NE):
                sp.dma_start(sent[bass.ds(rows[e], P), :], pad_rec[:, e, :]).then_inc(sem("pad_st"), 16)
            sp.wait_ge(sem("sent_st"), 16 * K * NT)
            sp.wait_ge(sem("pad_st"), 16 * NE)
            sp.wait_ge(sem("spare_st"), 16)
            sp.wait_ge(sem("table_ok"), 1)

            def load_tiles(it, first):
                rows = table_values(row_of[0:1, at(it, RING, RING)], NE * CAP + (SPARE - NE) * P,
                                    "a tile's rows are in its expert's region or the spare tiles after the last")
                for k in range(RING):
                    if not first:
                        sp.wait_ge(back_st[k], 16 * it)
                    sp.dma_start(got[:, k, :], sent[bass.ds(rows[k], P), :]).then_inc(got_ld[k], 16)

            load_tiles(0, True)
            with sp.Fori(1, TILES // RING) as it:
                load_tiles(it, False)

            for k in range(RING):
                sp.wait_ge(back_st[k], 16 * (TILES // RING))
            def load_results(g):
                for r in range(K):
                    sp.dma_start(zz[:, g % 4, r], back_groups[r, g]).then_inc(zz_ld[g % 4], 16)

            for g in range(4):
                load_results(g)
            for g in range(NG + 2):
                if g + 4 < NG:
                    sp.wait_ge(sem("z_sum"), g + 1)
                    load_results(g + 4)
                if g >= 2:
                    sp.wait_ge(sem("y_out_done"), g - 1)
                    sp.dma_start(out_groups[g - 2], y_out[:, g % 2]).then_inc(out_st[g % 2], 16)
            for k in range(2):
                sp.wait_ge(out_st[k], 16 * (NG // 2))

        @block.tensor
        def _(pe):
            mm = nc.tensor.matmul

            def x_transpose(b):
                pe.wait_ge(sem("xn_done"), b + 1)
                for t in range(T):
                    last = nc.tensor.transpose(M[:, t * P:(t + 1) * P], xn[:, t, :], ident[:])
                last.then_inc(sem("xt_mm"), 1)

            pe.wait_ge(sem("ident_ok"), 1)
            x_transpose(0)

            for src, loaded, banks in ((wq_in, "wq_ld", (S1[0], S1[1])), (wk_in, "wk_ld", (S0, PT0))):
                pe.wait_ge(sem(loaded), 16)
                for c in range(NP):
                    last = nc.tensor.transpose(banks[c // 4][:, (c % 4) * P:(c % 4 + 1) * P],
                                               src[:, 2 * c:2 * c + 2, :].rearrange("p h e -> p (h e)"), ident[:])
                last.then_inc(sem("wT_mm"), 1)
            pe.wait_ge(sem("wT_sb"), 2)
            for h in range(H):
                r = E * (h % 2)
                last = mm(m_banks[h // 8][h % 2][:, (h % 8 // 2) * P:(h % 8 // 2 + 1) * P],
                          wqT[r:r + E, h // 2, :], wkT[r:r + E, h // 2, :], start=True, stop=True)
                if h % 8 == 7:
                    last.then_inc(sem("m_mm"), 1)

            def product3(dst, a_hi, a_lo, b_hi, b_lo, start=True):
                mm(dst, a_hi, b_hi, start=start, stop=False, skip_group_check=True)
                mm(dst, a_hi, b_lo, start=False, stop=False, skip_group_check=True)
                return mm(dst, a_lo, b_hi, start=False, stop=True, skip_group_check=True)

            def y_proj(c):
                for k in range(2):
                    h = 2 * c + k
                    last = product3(M[:, k * S:(k + 1) * S], m_hi[:, h, :], m_lo[:, h, :],
                                    xt_hi[:], xt_lo[:], start=(k == 0))
                last.then_inc(y_mm, 1)

            def v_proj(t, half_of_heads):
                cols = slice(half_of_heads * 512, half_of_heads * 512 + 512)
                ts = slice(t * P, (t + 1) * P)
                product3(M[:, :], xt_hi[:, ts], xt_lo[:, ts], wv_hi[:, cols], wv_lo[:, cols]).then_inc(v_mm, 1)

            def scores(c):
                bk = S1[c % 2]
                for k in range(2):
                    product3(bk[:, k * S:(k + 1) * S], yq_hi[:, k, :], yq_lo[:, k, :], xs_hi[:], xs_lo[:],
                             start=(k == 0))
                for k in range(2):
                    last = mm(bk[:, k * S + P:(k + 1) * S], ident_bf[:], mask[:], start=False, stop=True,
                              skip_group_check=True)
                last.then_inc(s1_mm, 1)

            def scores0():
                for k in range(2):
                    mm(S0[:, k * P:(k + 1) * P], yq[:, k, 0:P], xt[:], start=(k == 0), stop=False,
                       skip_group_check=True)
                for k in range(2):
                    last = mm(S0[:, k * P:(k + 1) * P], ident_bf[:], mask[:], start=False, stop=True,
                              skip_group_check=True)
                last.then_inc(s0_mm, 1)

            def pv(c):
                for t, src, cols in ((0, pT0, slice(0, S)), (1, pT1, slice(P, S))):
                    for k in range(2):
                        h = 2 * c + k
                        last = mm(O[k * E:(k + 1) * E, cols], v_sb[:, t, h * E:(h + 1) * E], src[:, k, :],
                                  start=(t == 0), stop=(t == 1), skip_group_check=True)
                last.then_inc(pv_mm, 1)

            def w_o(c):
                for t in range(T):
                    last = mm(A[:, t * D:(t + 1) * D], hT[:, t * P:(t + 1) * P], wo_sb[:, c, :],
                              start=(c == 0 and t == 0), stop=(c == NP - 1), skip_group_check=True)
                if c == NP - 1:
                    last.then_inc(sem("wo_mm"), 1)

            def p_transpose(par):
                for k in range(2):
                    nc.tensor.transpose(PT0[:, k * S:k * S + P], prob[:, par, k, 0:P], ident[:])
                    last = nc.tensor.transpose(PT0[:, k * S + P:(k + 1) * S], prob[:, par, k, P:2 * P], ident[:])
                last.then_inc(t0_mm, 1)
                for k in range(2):
                    last = nc.tensor.transpose(PT1[:, k * P:(k + 1) * P], prob[:, par, k, 2 * P:3 * P], ident[:])
                last.then_inc(t1_mm, 1)

            pe.wait_ge(sem("xt_st"), 1)
            pe.wait_ge(sem("xt_split"), 1)
            pe.wait_ge(sem("m_split"), 2)
            y_proj(0)
            pe.wait_ge(sem("wv_ok"), 1)
            pe.wait_ge(y_sb, 1)
            v_proj(0, 0)
            pe.wait_ge(sem("xt_ok"), 1)
            pe.wait_ge(sem("mask_ok"), 1)
            scores0()
            pe.wait_ge(y_lo, 1)
            pe.wait_ge(sem("xs_ok"), 1)
            scores(0)
            pe.wait_ge(v_done, 1)
            v_proj(1, 0)
            pe.wait_ge(sem("m_split"), 4)
            pe.wait_ge(v_done, 2)
            y_proj(1)
            pe.wait_ge(sem("wo_ld"), 16)

            def batch(b):
                for j in range(NP):
                    p = NP * b + j
                    first = isinstance(b, int) and b == 0
                    nxt = there(b) if j < NP - 1 else there(b, -1)
                    nxt2 = there(b) if j < NP - 2 else there(b, -1)
                    last1 = there(b, 1) if j < 1 else there(b)
                    last2 = there(b, 1) if j < 2 else there(b)
                    if nxt and there(b):
                        pe.wait_ge(y_sb, p + 2)
                        if j == NP - 1:
                            pe.wait_ge(sem("xt_ok"), b + 2)
                        pe.wait_ge(ex0, p + 1)
                        scores0()
                        pe.wait_ge(y_lo, p + 2)
                        if j == NP - 1:
                            pe.wait_ge(sem("xs_ok"), b + 2)
                        if not (first and j == 0):
                            pe.wait_ge(ex1, p)
                        scores((j + 1) % 2)
                    if nxt2 and there(b):
                        if j in (0, 1, 2, 7) and not (first and j == 0):
                            pe.wait_ge(v_done, 4 * b + (5 if j == 7 else j + 2))
                        if j == 5 and there(b, -1):
                            pe.wait_ge(sem("xt_st"), b + 2)
                        if j == 6:
                            pe.wait_ge(sem("xt_split"), b + 2)
                        if there(b, 2):
                            if j == 3:
                                pe.wait_ge(sem("xfT_sb"), b - 1)
                            if j == 4:
                                pe.wait_ge(sem("lg_done"), b - 1)
                        y_proj((j + 2) % NP)
                    if last2:
                        pe.wait_ge(o_sb, p - 1)
                        if j == 2 and not first:
                            pe.wait_ge(sem("att_done"), b)
                        w_o((j - 2) % NP)
                    if last1:
                        pe.wait_ge(pt0_sb, p)
                        pe.wait_ge(pt1_sb, p)
                        if not (first and j == 1):
                            pe.wait_ge(o_sb, p - 1)
                        if j == 1:
                            pe.wait_ge(v_done, 4 * b + 2)
                        if j == 5:
                            pe.wait_ge(v_done, 4 * b + 4)
                        pv((j - 1) % NP)
                    extra = there(b) and (j in (0, 1) or (j in (4, 6, 7) and there(b, -1)))
                    router = there(b, 2) and j in (2, 3)
                    if (extra or router) and nxt2 and there(b):
                        pe.wait_ge(y_sb, p + 3)
                    if extra:
                        if j in (0, 1):
                            v_proj(j, 1)
                        elif j == 4:
                            x_transpose(b + 1)
                        else:
                            v_proj(j - 6, 0)
                    if router and j == 2:
                        pe.wait_ge(sem("xf_done"), b - 1)
                        for t in range(T):
                            last = nc.tensor.transpose(M[:, t * P:(t + 1) * P], xf[:, t, :], ident[:])
                        last.then_inc(sem("xfT_mm"), 1)
                    if router and j == 3:
                        pe.wait_ge(sem("xfT_sb"), b - 1)
                        for t in range(T):
                            last = mm(M[:, t * NE:(t + 1) * NE], xfT[:, t * P:(t + 1) * P], rw_sb[:],
                                      start=(t == 0), stop=True, skip_group_check=True)
                        last.then_inc(sem("logit_mm"), 1)
                    if there(b):
                        pe.wait_ge(nrm, p + 1)
                        if not (first and j == 0):
                            pe.wait_ge(pt0_sb, p)
                            pe.wait_ge(pt1_sb, p)
                    if there(b, 2) and j == 6:
                        if not there(b):
                            pe.wait_ge(pt1_sb, NP * B)
                            pe.wait_ge(sem("before_sb"), b - 2)
                        rows_before(b - 2)
                    if there(b):
                        p_transpose(j % 2)

            def rows_before(r):
                pe.wait_ge(sem("sel_ok"), r + 1)
                c = 2 * P
                groups = [(0, [(earlier, 0)]), (1, [(earlier, 1), (ones_bf, 0)]), (2, [(ones_bf, 0), (ones_bf, 1)])]
                for g, terms in groups:
                    for n, (lhs, t) in enumerate(terms):
                        last = mm(PT1[:, c + g * NE:c + (g + 1) * NE], lhs[:], sel_bf[:, t, :],
                                  start=(g == 0), stop=(n == len(terms) - 1), skip_group_check=True)
                last.then_inc(sem("before_mm"), 1)

            over_batches(batch)(pe)

            up_bank, out_bank = (S1[0], S1[1]), (O, M)
            w1h = w1_hi[:].rearrange("p e f -> p (e f)")
            w1l = w1_lo[:].rearrange("p e f -> p (e f)")
            w2f = w2_sb[:].rearrange("p e c d -> p (e c d)")
            assert F == NF * D
            pe.wait_ge(sem("w1_ok"), 1)
            pe.wait_ge(sem("ffn_ld"), 16 * (NE + 1))
            pe.wait_ge(sem("table_ok"), 1)

            def experts(it):
                return nc.values_load_multi_w_load_instructions(
                    expert_of[0:1, at(it, RING, RING + 2)], engines=[mybir.EngineType.PE], min_val=0,
                    max_val=(NE - 1) * F,
                    skip_runtime_bounds_check_because="the table's entries are clamped to the last expert")[1]

            def rows_T(n, k, it, first):
                pe.wait_ge(got_ld[k], 16 * (it + 1))
                if not first:
                    pe.wait_ge(sem("g_split"), n)
                nc.tensor.transpose(PT1[:, 0:P], got[:, k, 0:D], ident[:]).then_inc(sem("gT_mm"), 1)

            def up(n, k, e, first):
                pe.wait_ge(sem("g_split"), n + 1)
                if not first:
                    pe.wait_ge(sem("gelu"), n - 1)
                c = bass.ds(e, F)
                product3(up_bank[k % 2][:, :], gT_hi[:, k % 2, :], gT_lo[:, k % 2, :], w1h[:, c], w1l[:, c])\
                    .then_inc(sem("up_mm"), 1)

            def hidden_T(n, k, first):
                pe.wait_ge(sem("gelu"), n + 1)
                if not first:
                    pe.wait_ge(sem("hidT_sb"), n)
                for c in range(NF):
                    last = nc.tensor.transpose(PT0[:, c * P:(c + 1) * P], hid[:, k % 2, c * P:(c + 1) * P], ident[:])
                last.then_inc(sem("hidT_mm"), 1)

            def down(n, k, e, first):
                pe.wait_ge(sem("hidT_sb"), n + 1)
                if not first:
                    pe.wait_ge(sem("yo_done"), n - 1)
                w2_e = w2f[:, bass.ds(e, F)]
                for c in range(NF):
                    last = mm(out_bank[k % 2][:, 0:D], hidT[:, k % 2, c * P:(c + 1) * P], w2_e[:, c * D:(c + 1) * D], start=(c == 0), stop=(c == NF - 1))
                last.then_inc(sem("out_mm"), 1)

            rows_T(0, 0, 0, True)
            rows_T(1, 1, 0, False)
            up(0, 0, experts(0)[1], True)

            def ring(it, first, last):
                e = experts(it)
                for k in range(RING):
                    n = it * RING + k
                    hidden_T(n, k, first and k == 0)
                    if not (last and k == RING - 1):
                        up(n + 1, (k + 1) % RING, e[k + 2], first and k == 0)
                    if not (last and k >= RING - 2):
                        rows_T(n + 2, (k + 2) % RING, it + (k + 2) // RING, False)
                    if not (first and k == 0):
                        down(n - 1, (k - 1) % RING, e[k], first and k <= 2)
                if last:
                    down(n, k, e[k + 1], False)

            ring(0, True, False)
            with pe.Fori(1, TILES // RING - 1) as it:
                ring(it, False, False)
            ring(TILES // RING - 1, False, True)

            for g in range(NG):
                pe.wait_ge(zz_ld[g % 4], 16 * K * (g // 4 + 1))
                if g >= 4:
                    pe.wait_ge(sem("zn_done"), g - 3)
                for r in range(K):
                    last = mm(sum_bank[g % 4][:], ident[:], zz[:, g % 4, r].rearrange("p t d -> p (t d)"),
                              start=(r == 0), stop=(r == K - 1))
                last.then_inc(sem("z_sum"), 1)

        @block.vector
        def _(dve):
            v = nc.vector

            def stats(kind, src, tiles, done):
                for t in range(tiles):
                    last = v.bn_stats(stat[kind][:, t, :], src[:, t, :])
                return last

            def moments(kind, tiles):
                for t in range(tiles):
                    last = v.bn_aggr(mv[kind][:, t, :], stat[kind][:, t, :])
                return last

            def normalise(kind, dst, src, tiles):
                for t in range(tiles):
                    last = v.tensor_scalar(dst[:, t, :], src[:, t, :], mv[kind][:, t, 0:1], rstd[kind][:, t:t + 1],
                                           ALU.subtract, ALU.mult)
                return last

            def layer_stats(kind, src, tiles, n):
                stats(kind, src, tiles, n)
                dve.drain()
                moments(kind, tiles).then_inc(sem(f"mv_{kind}"), 1)

            dve.wait_ge(sem("x_in_ld"), 16)
            layer_stats("x", x_in, T, 1)
            def xs_copy():
                v.tensor_copy(xt[:], xt_st[:, 0:P])
                v.tensor_copy(xs_lo[:], xt_lo[:].bitcast(F32)).then_inc(sem("xt_ok"), 1)

            def x_split(b):
                dve.wait_ge(sem("xt_st"), b + 1)
                v.tensor_copy(xt_hi[:], xt_st[:]).then_inc(sem("xt_h"), 1)
                dve.wait_ge(sem("xt_h"), b + 1)
                v.tensor_tensor(xt_lo[:], xt_st[:], xt_hi[:].bitcast(F32), ALU.subtract).then_inc(sem("xt_split"), 1)

            def y_low(p):
                dve.wait_ge(y_h, p + 1)
                v.tensor_tensor(yq_lo[:], yq[:, :, P:S], yq_hi[:].bitcast(F32), ALU.subtract).then_inc(y_lo, 1)

            def maxima0(p, par):
                dve.wait_ge(s0_mm, p + 1)
                v.tensor_reduce(nmax[:, par, 2:4], S0[:, 0:2 * P].rearrange("p (k t) -> p k t", k=2), AX_X, ALU.max,
                                negate=True).then_inc(mx0, 1)

            def maxima1(p, par):
                dve.wait_ge(s1_mm, p + 1)
                v.tensor_reduce(nmax[:, par, 0:2], S1[par][:].rearrange("p (k t) -> p k t", k=2), AX_X, ALU.max,
                                negate=True).then_inc(mx1, 1)

            dve.wait_ge(sem("rstd_x"), 1)
            normalise("x", xn, x_in, T).then_inc(sem("xn_done"), 1)
            x_split(0)
            dve.wait_ge(sem("xt_split"), 1)
            xs_copy()
            dve.wait_ge(sem("wT_mm"), 2)
            v.tensor_copy(wkT[:, 0:4, :], S0[:].rearrange("p (c d) -> p c d", c=4))
            v.tensor_copy(wkT[:, 4:8, :], PT0[:].rearrange("p (c d) -> p c d", c=4)).then_inc(sem("wT_sb"), 1)
            dve.wait_ge(sem("wv_ld"), 16)
            v.tensor_copy(wv_hi[:], wv_in[:]).then_inc(sem("wv_h"), 1)
            dve.wait_ge(sem("wv_h"), 1)
            v.tensor_tensor(wv_lo[:], wv_in[:], wv_hi[:].bitcast(F32), ALU.subtract).then_inc(sem("wv_ok"), 1)
            for n in range(4):
                g, i = n // 2, n % 2
                dve.wait_ge(sem("m_h"), n + 1)
                v.scalar_tensor_tensor(m_part(m_lo, g, i), m_banks[g][i][:].rearrange("p (c d) -> p c d", c=4),
                                       float(E) ** -0.5, m_part(m_hi, g, i).bitcast(F32), ALU.mult,
                                       ALU.subtract).then_inc(sem("m_split"), 1)
            y_low(0)
            maxima0(0, 0)
            maxima1(0, 0)
            y_low(1)

            def batch(b):
                for j in range(NP):
                    p = NP * b + j
                    par = j % 2
                    if there(b):
                        dve.wait_ge(ex1, p + 1)
                        v.reciprocal(rden[:, par, :], den[:, par, :]).then_inc(rc, 1)
                        if j < NP - 1 or there(b, -1):
                            maxima0(p + 1, (j + 1) % 2)
                        dve.wait_ge(rc, p + 1)
                        for k in range(2):
                            v.tensor_scalar(prob[:, par, k, P:3 * P], prob[:, par, k, P:3 * P],
                                            rden[:, par, k:k + 1], None, ALU.mult)
                            q = v.tensor_scalar(prob[:, par, k, 0:P], prob[:, par, k, 0:P],
                                                rden[:, par, 2 + k:3 + k], None, ALU.mult)
                        q.then_inc(nrm, 1)
                        if j < NP - 1 or there(b, -1):
                            maxima1(p + 1, (j + 1) % 2)
                    if there(b) and (j < NP - 2 or there(b, -1)):
                        y_low(p + 2)
                    if there(b, 1):
                        if there(b):
                            tail(b - 1, j)
                        elif j != 6:
                            tail(b - 1, 6 if j == 5 else j)
                    if there(b) and there(b, -1):
                        ahead(b + 1, j)
                    if there(b, 2):
                        router(b - 2, j)
                    if there(b, 2) and j == NP - 1:
                        dispatch(b - 2)
                    if there(b, 2) and j == 6:
                        if there(b):
                            dve.wait_ge(t1_mm, p + 1)
                        dve.wait_ge(sem("before_mm"), b - 1)
                        v.tensor_copy(before[:, 0:(T + 1) * NE], PT1[:, 2 * P:2 * P + (T + 1) * NE])\
                            .then_inc(sem("before_sb"), 1)
                    if there(b):
                        dve.wait_ge(t1_mm, p + 1)
                        v.tensor_copy(pT1[:], PT1[:, 0:2 * P].rearrange("p (k s) -> p k s", k=2)).then_inc(pt1_sb, 1)

            def over_e(a):
                return a.unsqueeze(2).broadcast_to([P, T, NE])

            def router(r, j):
                if j == 0:
                    rows = x1[:, at(r, T, T), :]
                    dve.wait_ge(sem("x1_done"), r + 1)
                    for t in range(T):
                        v.bn_stats(stat["f"][:, t, :], rows[:, t, :])
                    dve.drain()
                    moments("f", T).then_inc(sem("mv_f"), 1)
                if j == 1:
                    rows = x1[:, at(r, T, T), :]
                    dve.wait_ge(sem("rstd_f"), r + 1)
                    if not (isinstance(r, int) and r == 0):
                        dve.wait_ge(sem("rec_ok"), r)
                    for t in range(T):
                        q = v.tensor_scalar(xf[:, t, :], rows[:, t, :], mv["f"][:, t, 0:1],
                                            rstd["f"][:, t:t + 1], ALU.subtract, ALU.mult)
                    q.then_inc(sem("xf_done"), 1)
                if j == 3:
                    logits = M[:, 0:T * NE].rearrange("p (t e) -> p t e", t=T)
                    dve.wait_ge(sem("logit_mm"), r + 1)
                    v.tensor_reduce(rmax[:], logits, AX_X, ALU.max)
                    dve.drain()
                    v.tensor_tensor(lg[:], logits, over_e(rmax[:]), ALU.subtract).then_inc(sem("lg_done"), 1)
                if j == 4:
                    dve.wait_ge(sem("rexp"), r + 1)
                    v.tensor_reduce(rsum[:], ex[:], AX_X, ALU.add)
                    dve.drain()
                    v.reciprocal(rrs[:], rsum[:])
                    dve.drain()
                    v.tensor_tensor(pr[:], ex[:], over_e(rrs[:]), ALU.mult)
                    dve.drain()
                    for t in range(T):
                        v.max(top[:, t, :], pr[:, t, :])
                    dve.drain()
                    for t in range(T):
                        v.max_index(topi[:, t, :], top[:, t, :], pr[:, t, :])
                if j == 5:
                    dve.drain()
                    v.tensor_copy(topf[:], topi[:])
                    dve.drain()
                    for k in range(K):
                        v.tensor_tensor(sel[k][:], iota_e[:], over_e(topf[:, :, k]), ALU.is_equal)
                    dve.drain()
                    v.tensor_tensor(sel_bf[:], sel[0][:], sel[1][:], ALU.add).then_inc(sem("sel_ok"), 1)
                if j == 6:
                    if not (isinstance(r, int) and r == 0):
                        dve.wait_ge(sem("sent_st"), 16 * K * T * r)
                    for k in range(K):
                        v.tensor_copy(rec[k][:, :, C_GATE], top[:, :, k])
                        v.tensor_copy(rec[k][:, :, C_ID].bitcast(I32), ids[:, k, :])

            def dispatch(r):
                dve.drain()
                v.tensor_scalar(ids[:], ids[:], float(S), None, ALU.add)
                v.tensor_tensor(place[:], before[:, 0:T * NE].rearrange("p (t e) -> p t e", t=T),
                                base[:].unsqueeze(1).broadcast_to([P, T, NE]), ALU.add)
                dve.drain()
                v.tensor_tensor(base[:], base[:], before[:, T * NE:(T + 1) * NE], ALU.add)
                for k in range(K):
                    v.tensor_tensor(picked[:, k], place[:], sel[k][:], ALU.mult)
                dve.drain()
                v.tensor_reduce(slot_f[:], picked[:], AX_X, ALU.add)
                dve.drain()
                v.tensor_copy(slot[:], slot_f[:]).then_inc(sem("slot_ok"), 1)

            def ahead(b, j):
                if j == 0:
                    dve.wait_ge(sem("x_in_ld"), 16 * b + 16)
                    layer_stats("x", x_in, T, b + 1)
                if j == 2:
                    dve.wait_ge(sem("rstd_x"), b + 1)
                    dve.wait_ge(sem("xn_kept"), b)
                    normalise("x", xn, x_in, T).then_inc(sem("xn_done"), 1)
                if j == 5:
                    dve.wait_ge(y_mm, NP * b)
                    x_split(b)
                if j == 6:
                    xs_copy()

            def tail(b, j):
                if j == 1:
                    dve.wait_ge(sem("wo_mm"), b + 1)
                    v.tensor_tensor(att[:], xn_res[:], A[:, 0:T * D].rearrange("p (t d) -> p t d", t=T), ALU.add)\
                        .then_inc(sem("att_done"), 1)
                    dve.wait_ge(sem("att_done"), b + 1)
                    layer_stats("a", att, T, b + 1)
                if j == 2:
                    dve.wait_ge(sem("rstd_a"), b + 1)
                    normalise("a", z1, att, T).then_inc(sem("z1_done"), 1)
                if j == 3:
                    dve.wait_ge(sem("z2_done"), b + 1)
                    layer_stats("z", z2, T, b + 1)
                if j == 6:
                    dve.wait_ge(sem("rstd_z"), b + 1)
                    normalise("z", z3, z2, T).then_inc(sem("z3_done"), 1)

            dve.wait_ge(sem("consts_ok"), 1)
            v.tensor_copy(base[:], base0[:])
            over_batches(batch)(dve)

            def over_tiles(a):
                return a.unsqueeze(1).broadcast_to([1, TILES, NE])

            dve.drain()
            v.tensor_copy(pad_row[:], base[0:1, :]).then_inc(sem("pads_known"), 1)
            v.tensor_tensor(cnt_f[:], base[0:1, :], base0[0:1, :], ALU.subtract)
            dve.drain()
            v.tensor_scalar(cnt_i[:], cnt_f[:], float(P - 1), None, ALU.add)
            dve.drain()
            v.tensor_scalar(cnt_i[:], cnt_i[:], P.bit_length() - 1, None, ALU.logical_shift_right)
            dve.drain()
            v.tensor_copy(n_tiles[:], cnt_i[:])
            dve.drain()
            v.tensor_tensor_scan(ends[:], ones_row[:], n_tiles[:], 0.0, ALU.mult, ALU.add)
            dve.drain()
            v.tensor_tensor(over, over_tiles(ends[:]), tile_no[:].unsqueeze(2).broadcast_to([1, TILES, NE]),
                            ALU.is_le)
            dve.drain()
            v.tensor_reduce(tile_e[:], over, AX_X, ALU.add)
            v.tensor_tensor(over_n, over, over_tiles(n_tiles[:]), ALU.mult)
            dve.drain()
            v.tensor_reduce(tile_s[:], over_n, AX_X, ALU.add)
            v.memset(expert_of[:], 0)
            dve.drain()
            v.tensor_scalar(expert_of[:, 1:TILES + 1], tile_e[:], float(NE - 1), float(F), ALU.min, ALU.mult)
            dve.drain()
            v.tensor_tensor(tile_s[:], tile_no[:], tile_s[:], ALU.subtract)
            v.tensor_scalar(tile_e[:], tile_e[:], float(CAP), None, ALU.mult)
            dve.drain()
            v.tensor_scalar(tile_s[:], tile_s[:], float(P), None, ALU.mult)
            dve.drain()
            v.tensor_tensor(tile_r[:], tile_s[:], tile_e[:], ALU.add)
            dve.drain()
            v.tensor_copy(row_of[:], tile_r[:]).then_inc(sem("table_ok"), 1)

            def split_rows(n, k):
                dve.wait_ge(sem("gT_mm"), n + 1)
                v.tensor_copy(gT_hi[:, k % 2, :], PT1[:, 0:P]).then_inc(sem("g_h"), 1)
                dve.wait_ge(sem("g_h"), n + 1)
                v.tensor_tensor(gT_lo[:, k % 2, :], PT1[:, 0:P], gT_hi[:, k % 2, :].bitcast(F32), ALU.subtract)\
                    .then_inc(sem("g_split"), 1)

            split_rows(0, 0)
            split_rows(1, 1)

            def ring(n0, last):
                for k in range(RING):
                    dve.wait_ge(sem("hidT_mm"), n0 + k + 1)
                    if not (isinstance(n0, int) and n0 == 0 and k < 2):
                        dve.wait_ge(sem("out_mm"), n0 + k - 1)
                    v.tensor_copy(hidT[:, k % 2, :], PT0[:]).then_inc(sem("hidT_sb"), 1)
                    if not (last and k >= RING - 2):
                        if isinstance(n0, int) and n0 == 0 and k == 0:
                            dve.wait_ge(sem("up_mm"), 1)
                        split_rows(n0 + k + 2, k)

            ring(0, False)
            with dve.Fori(1, TILES // RING - 1) as it:
                ring(it * RING, False)
            ring(TILES - RING, True)

            for g in range(NG + 2):
                if g < NG:
                    o = f"o{g % 2}"
                    dve.wait_ge(sem("z_sum"), g + 1)
                    for t in range(GT):
                        v.bn_stats(stat[o][:, t, :], sum_bank[g % 4][:, t * D:(t + 1) * D])
                    dve.drain()
                    if g >= 2:
                        dve.wait_ge(sem("zn_done"), g - 1)
                    for t in range(GT):
                        q = v.bn_aggr(mv[o][:, t, :], stat[o][:, t, :])
                    q.then_inc(sem("mv_o"), 1)
                if 1 <= g <= NG:
                    h = g - 1
                    o = f"o{h % 2}"
                    dve.wait_ge(sem("rstd_o"), h + 1)
                    v.scalar_tensor_tensor(shift[:, h % 2, :], mv[o][:, :, 0], -1.0, rstd[o][:], ALU.mult, ALU.mult)\
                        .then_inc(sem("shift_ok"), 1)
                if g >= 2:
                    h = g - 2
                    dve.wait_ge(sem("zn_done"), h + 1)
                    if h >= 2:
                        dve.wait_ge(out_st[h % 2], 16 * (h // 2))
                    v.tensor_tensor(y_out[:, h % 2], x1[:, h * GT:(h + 1) * GT, :], zn[:, h % 2], ALU.add)\
                        .then_inc(sem("y_out_done"), 1)

        @block.scalar
        def _(act):
            a = nc.scalar
            def xt_copy(b):
                act.wait_ge(sem("xt_mm"), b + 1)
                a.activation(xt_st[:], M[:, 0:S], ACT.Copy).then_inc(sem("xt_st"), 1)

            def y_copy(p):
                act.wait_ge(y_mm, p + 1)
                a.activation(yq[:], M[:].rearrange("p (k s) -> p k s", k=2), ACT.Copy).then_inc(y_sb, 1)
                act.wait_ge(y_sb, p + 1)
                a.activation(yq_hi[:], yq[:, :, P:S], ACT.Copy).then_inc(y_h, 1)

            def xs_copy(b):
                act.wait_ge(sem("xt_split"), b + 1)
                a.activation(xs_hi[:], xt_hi[:].bitcast(F32), ACT.Copy).then_inc(sem("xs_ok"), 1)

            def exps(p, par):
                act.wait_ge(mx0, p + 1)
                for k in range(2):
                    q = a.activation(prob[:, par, k, 0:P], S0[:, k * P:(k + 1) * P], ACT.Exp,
                                     bias=nmax[:, par, 2 + k:3 + k], accum_out=den[:, par, 2 + k:3 + k])
                q.then_inc(ex0, 1)
                act.wait_ge(mx1, p + 1)
                for k in range(2):
                    q = a.activation(prob[:, par, k, P:3 * P], S1[par][:, k * S:(k + 1) * S], ACT.Exp,
                                     bias=nmax[:, par, k:k + 1], accum_out=den[:, par, k:k + 1])
                q.then_inc(ex1, 1)

            def v_copy(n, t, half_of_heads):
                act.wait_ge(v_mm, n)
                a.activation(v_sb[:, t, half_of_heads * 512:half_of_heads * 512 + 512], M[:], ACT.Copy)\
                    .then_inc(v_done, 1)

            def o_copy(p):
                act.wait_ge(pv_mm, p + 1)
                a.activation(hT[:], O[:, 0:S], ACT.Copy).then_inc(o_sb, 1)

            xt_copy(0)
            xs_copy(0)
            act.wait_ge(sem("wT_mm"), 1)
            a.activation(wqT[:, 0:4, :], S1[0][:].rearrange("p (c d) -> p c d", c=4), ACT.Copy)
            a.activation(wqT[:, 4:8, :], S1[1][:].rearrange("p (c d) -> p c d", c=4), ACT.Copy)\
                .then_inc(sem("wT_sb"), 1)
            for n in range(4):
                g, i = n // 2, n % 2
                act.wait_ge(sem("m_mm"), g + 1)
                a.activation(m_part(m_hi, g, i), m_banks[g][i][:].rearrange("p (c d) -> p c d", c=4), ACT.Copy,
                             scale=float(E) ** -0.5).then_inc(sem("m_h"), 1)
            y_copy(0)
            v_copy(1, 0, 0)
            v_copy(2, 1, 0)
            exps(0, 0)
            y_copy(1)

            def batch(b):
                for j in range(NP):
                    p = NP * b + j
                    first = isinstance(b, int) and b == 0
                    if there(b):
                        if j < NP - 2 or there(b, -1):
                            y_copy(p + 2)
                        if j < NP - 1 or there(b, -1):
                            if not (first and j == 0):
                                act.wait_ge(t1_mm, p)
                            exps(p + 1, (j + 1) % 2)
                        if j == 6 and there(b, -1):
                            xs_copy(b + 1)
                    if (there(b) and not (first and j == 0)) or (j == 0 and there(b, 1)):
                        o_copy(p - 1)
                    if there(b):
                        if there(b, -1) and j == 4:
                            act.wait_ge(sem("xt_ok"), b + 1)
                            xt_copy(b + 1)
                        if j in (0, 1):
                            v_copy(4 * b + 3 + j, j, 1)
                        if there(b, -1) and j in (6, 7):
                            v_copy(4 * b + j - 1, j - 6, 0)
                    if there(b, 2):
                        if j == 2:
                            act.wait_ge(sem("xfT_mm"), b - 1)
                            a.activation(xfT[:], M[:, 0:S], ACT.Copy).then_inc(sem("xfT_sb"), 1)
                        if j == 3:
                            act.wait_ge(sem("lg_done"), b - 1)
                            a.activation(ex[:], lg[:], ACT.Exp).then_inc(sem("rexp"), 1)
                        if j == 5:
                            if there(b, 3):
                                act.wait_ge(sem("sent_st"), 16 * K * T * (b - 2))
                            for k in range(K):
                                q = a.activation(rec[k][:, :, 0:D], xf[:], ACT.Copy)
                            q.then_inc(sem("rec_ok"), 1)
                    if there(b):
                        act.wait_ge(t0_mm, p + 1)
                        a.activation(pT0[:], PT0[:].rearrange("p (k s) -> p k s", k=2), ACT.Copy)\
                            .then_inc(pt0_sb, 1)

            over_batches(batch)(act)

            def gelu(n, k, first):
                act.wait_ge(sem("up_mm"), n + 1)
                if not first:
                    act.wait_ge(sem("hidT_mm"), n - 1)
                a.activation(hid[:, k % 2, :], S1[k % 2][:], ACT.Gelu_apprx_tanh).then_inc(sem("gelu"), 1)

            def gated(n, k, first, it, step):
                act.wait_ge(sem("out_mm"), n + 1)
                if not first:
                    act.wait_ge(back_st[k], 16 * (it if step > 0 else it - 1))
                a.activation(yo[:, k, :], (O, M)[k % 2][:, 0:D], ACT.Copy, scale=got[:, k, C_GATE:C_GATE + 1])\
                    .then_inc(sem("yo_done"), 1)

            def ring(it, first, last):
                for k in range(RING):
                    n = it * RING + k
                    if not (last and k == RING - 1):
                        gelu(n + 1, (k + 1) % RING, first and k == 0)
                    if not (first and k == 0):
                        gated(n - 1, (k - 1) % RING, first or (isinstance(it, int) and it == 1 and k == 0), it, k)
                if last:
                    gated(n, k, False, it, k + 1)

            gelu(0, 0, True)
            ring(0, True, False)
            ring(1, False, False)
            with act.Fori(2, TILES // RING - 1) as it:
                ring(it, False, False)
            ring(TILES // RING - 1, False, True)

            for g in range(NG):
                h = g % 2
                act.wait_ge(sem("shift_ok"), g + 1)
                if g >= 2:
                    act.wait_ge(sem("y_out_done"), g - 1)
                for t in range(GT):
                    last_op = a.activation(zn[:, h, t, :], sum_bank[g % 4][:, t * D:(t + 1) * D], ACT.Identity,
                                           bias=shift[:, h, t:t + 1], scale=rstd[f"o{h}"][:, t:t + 1])
                last_op.then_inc(sem("zn_done"), 1)

        @block.gpsimd
        def _(pool):
            q = nc.gpsimd
            q.memset(ident[:], 0.0)
            q.memset(half[:], -0.5)
            q.memset(ln_eps[:], LN_EPS)
            q.memset(att_eps[:], ATT_EPS)
            q.memset(mask[:], 0.0).then_inc(sem("p_set"), 1)
            pool.wait_ge(sem("p_set"), 1)
            q.affine_select(out=ident[:], in_=ident[:], compare_op=ALU.not_equal, fill=1.0, base=0,
                            pattern=[[-1, P]], channel_multiplier=1).then_inc(sem("ident_ok"), 1)
            pool.wait_ge(sem("ident_ok"), 1)
            q.tensor_copy(ident_bf[:], ident[:])
            q.affine_select(out=mask[:], in_=mask[:], compare_op=ALU.is_ge, fill=MASKED, base=0,
                            pattern=[[-1, P]], channel_multiplier=1).then_inc(sem("mask_ok"), 1)
            q.memset(ones_bf[:], 1.0)
            q.memset(earlier[:], 1.0)
            q.memset(ones_row[:], 1.0)
            q.memset(pad_rec[:], 0.0)
            for r in rec:
                q.memset(r[:], 0.0)
            q.iota(iota_e[:], pattern=[[0, T], [1, NE]], base=0, channel_multiplier=0,
                   allow_small_or_imprecise_dtypes=True)
            q.iota(ids[:], pattern=[[N, K], [P, T]], base=0, channel_multiplier=1,
                   allow_small_or_imprecise_dtypes=True)
            q.iota(base0[:], pattern=[[CAP, NE]], base=0, channel_multiplier=0,
                   allow_small_or_imprecise_dtypes=True)
            q.iota(tile_no[:], pattern=[[1, TILES]], base=0, channel_multiplier=0,
                   allow_small_or_imprecise_dtypes=True).then_inc(sem("iota_ok"), 1)
            pool.wait_ge(sem("iota_ok"), 1)
            q.affine_select(out=earlier[:], in_=earlier[:], compare_op=ALU.is_gt, fill=0.0, base=0,
                            pattern=[[1, P]], channel_multiplier=-1).then_inc(sem("consts_ok"), 1)
            q.iota(pad_rec[:, :, C_ID].bitcast(I32), pattern=[[P, SPARE]], base=K * N, channel_multiplier=1)\
                .then_inc(sem("pad_ok"), 1)

            def inverse_root(kind, tiles, eps, n):
                pool.wait_ge(sem(f"mv_{kind}"), n)
                q.tensor_tensor(ve[kind][:, 0:tiles], mv[kind][:, 0:tiles, 1], eps[:, 0:tiles], ALU.add)\
                    .then_inc(sem(f"ve_{kind}"), 1)
                pool.wait_ge(sem(f"ve_{kind}"), n)
                q.tensor_tensor(rstd[kind][:, 0:tiles], ve[kind][:, 0:tiles], half[:, 0:tiles], ALU.pow)\
                    .then_inc(sem(f"rstd_{kind}"), 1)

            inverse_root("x", T, ln_eps, 1)
            pool.wait_ge(sem("gb_ld"), 16 * 2 * T)
            pool.wait_ge(sem("xn_done"), 1)
            q.tensor_copy(xn_res[:], xn[:]).then_inc(sem("xn_kept"), 1)
            pool.wait_ge(sem("w1_ld"), 16)
            q.tensor_copy(w1_hi[:], w1_in[:]).then_inc(sem("w1_h"), 1)
            pool.wait_ge(sem("w1_h"), 1)
            q.tensor_tensor(w1_lo[:], w1_in[:], w1_hi[:].bitcast(F32), ALU.subtract).then_inc(sem("w1_ok"), 1)

            def tail(b):
                inverse_root("a", T, att_eps, b + 1)
                if not (isinstance(b, int) and b == B - 1):
                    q.tensor_copy(xn_res[:], xn[:]).then_inc(sem("xn_kept"), 1)
                pool.wait_ge(sem("z1_done"), b + 1)
                q.tensor_tensor(z2[:], z1[:], gamma_t[:], ALU.mult).then_inc(sem("z_g"), 1)
                pool.wait_ge(sem("z_g"), b + 1)
                q.tensor_tensor(z2[:], z2[:], beta_t[:], ALU.add).then_inc(sem("z2_done"), 1)

            def tail_end(b):
                inverse_root("z", T, ln_eps, b + 1)
                pool.wait_ge(sem("z3_done"), b + 1)
                pool.wait_ge(sem("x_res_ld"), 16 * b + 16)
                q.tensor_tensor(x1[:, at(b, T, T), :], x_res[:], z3[:], ALU.add).then_inc(sem("x1_done"), 1)

            def send(r):
                pool.wait_ge(sem("slot_ok"), r + 1)
                pool.wait_ge(sem("rec_ok"), r + 1)
                q.sem_inc(sem("send_turn"), 1)
                for k in range(K):
                    for t in range(T):
                        q.indirect_dma_start(sent, bass.IndirectOffsetOnAxis(ap=slot[:, k, t:t + 1], axis=0),
                                             rec[k][:, t, :], None).then_inc(sem("sent_st"), 16)

            def batch(b):
                if there(b) and there(b, -1):
                    inverse_root("x", T, ln_eps, b + 2)
                if there(b, 2):
                    inverse_root("f", T, ln_eps, b - 1)
                if there(b, 1):
                    tail(b - 1)
                    tail_end(b - 1)
                if isinstance(b, int) and b == B + 1:
                    send(b - 3)
                if there(b, 2) and not (isinstance(b, int) and b == B):
                    send(b - 2)

            over_batches(batch)(pool)

            def store(n, k):
                pool.wait_ge(sem("yo_done"), n + 1)
                q.sem_inc(sem("store_turn"), 1)
                q.indirect_dma_start(back, bass.IndirectOffsetOnAxis(ap=got[:, k, C_ID:C_ID + 1].bitcast(I32), axis=0),
                                     yo[:, k, :], None).then_inc(back_st[k], 16)

            with pool.Fori(0, TILES // RING) as it:
                for k in range(RING):
                    store(it * RING + k, k)

            for g in range(NG):
                o = f"o{g % 2}"
                pool.wait_ge(sem("mv_o"), g + 1)
                q.tensor_tensor(ve[o][:], mv[o][:, :, 1], ln_eps[:], ALU.add).then_inc(sem("ve_o"), 1)
                pool.wait_ge(sem("ve_o"), g + 1)
                q.tensor_tensor(rstd[o][:], ve[o][:], half[:], ALU.pow).then_inc(sem("rstd_o"), 1)



_INS = ["L0_attn_x", "L0_attn_Wq", "L0_attn_Wk", "L0_attn_Wv", "L0_attn_Wo", "L0_attn_gamma", "L0_attn_beta",
        "L0_ffn_router_w", "L0_ffn_w1", "L0_ffn_w2"]


def kernel(**inputs):
    import numpy as np
    import concourse.bacc as bacc
    from concourse.bass_utils import run_bass_kernel_spmd

    nc = bacc.Bacc("TRN2", target_bir_lowering=False, num_devices=1)
    arrays, args = {}, []
    for name in _INS:
        a = np.ascontiguousarray(inputs[name])
        arrays[name] = a
        args.append(nc.dram_tensor(name, a.shape, mybir.dt.from_np(a.dtype), kind="ExternalInput").ap())
    out = nc.dram_tensor("out", arrays["L0_attn_x"].shape, F32, kind="ExternalOutput").ap()
    sandwich_kernel(nc, *args, out)
    r = run_bass_kernel_spmd(nc, [arrays], core_ids=[0])
    return r.results[0]["out"]
```

```python
from contextlib import ExitStack

import concourse.bass as bass
from concourse import mybir

ALU = mybir.AluOpType
ACT = mybir.ActivationFunctionType
F32 = mybir.dt.float32
F32R = mybir.dt.float32r
BF16 = mybir.dt.bfloat16
U32 = mybir.dt.uint32
I32 = mybir.dt.int32
AX_X = mybir.AxisListType.X

P = 128
LN_EPS = 1e-5
ATT_EPS = 1e-3
MASKED = -3.0e38


def sandwich_kernel(nc, x, wq, wk, wv, wo, gamma, beta, router_w, w1, w2, out):
    B, S, D = x.shape
    H, _, E = wq.shape
    NE, _, F = w1.shape
    T = S // P
    NP = H // 2
    NF = F // P
    NT = B * T
    GT = 4
    NG = NT // GT
    N = NT * P
    K = 2
    CAP = N + P
    TILES = K * NT + NE
    RING = 8
    EARLY = 3 * RING
    LATE = TILES - EARLY
    assert EARLY <= K * T * (B - 3) - NE
    REC = D + 4
    C_ID, C_GATE = D, D + 1
    SPARE = NE + TILES - K * NT
    assert (D, E, T, NP, F) == (P, P // 2, 2, 8, 512) and NT % GT == 0 and TILES % RING == 0

    x_tiles = x.rearrange("b (t p) d -> b p t d", p=P)
    sent = nc.dram_tensor("sent_rows", ((NE + 1) * CAP, REC), F32, kind="Internal").ap()
    back = nc.dram_tensor("expert_rows", (K * N + SPARE * P, D), F32, kind="Internal").ap()
    back_groups = back[0:K * N, :].rearrange("(r g k p) d -> r g p k d", r=K, k=GT, p=P)
    out_groups = out.rearrange("b (t p) d -> p (b t) d", p=P).rearrange("p (g k) d -> g p k d", k=GT)

    with ExitStack() as ctx:
        def sb(name, shape, dt=F32):
            return ctx.enter_context(nc.sbuf_tensor(name, shape, dt))

        def bank(name):
            return ctx.enter_context(nc.psum_tensor(name, [P, 512], F32))

        sems = {}

        def sem(name):
            if name not in sems:
                sems[name] = ctx.enter_context(nc.semaphore(name))
            return sems[name]

        wqk_in = sb("wqk_in", [P, 2, H, E])
        wq_in, wk_in = wqk_in[:, 0], wqk_in[:, 1]
        wqT = sb("wqT", [P, NP, P])
        wkT = sb("wkT", [P, NP, P])
        m_hi = sb("m_hi", [P, H, P], F32R)
        m_lo = sb("m_lo", [P, H, P], F32R)
        wv_in = sb("wv_in", [P, H * E])
        wv_hi = sb("wv_hi", [P, H * E], F32R)
        wv_lo = sb("wv_lo", [P, H * E], F32R)
        wo_sb = sb("wo_sb", [P, NP, D])
        w1_in = sb("w1_in", [P, NE, F])
        w1_hi = sb("w1_hi", [P, NE, F], F32R)
        w1_lo = sb("w1_lo", [P, NE, F], F32R)
        w2_sb = sb("w2_sb", [P, NE, NF, D])
        rw_sb = sb("rw_sb", [P, NE])
        gamma_t = sb("gamma_t", [P, T, D])
        beta_t = sb("beta_t", [P, T, D])
        ident = sb("ident", [P, P])
        ident_bf = sb("ident_bf", [P, P], BF16)
        mask = sb("mask", [P, P], BF16)
        half = sb("half", [P, GT])
        ln_eps = sb("ln_eps", [P, GT])
        att_eps = sb("att_eps", [P, GT])

        x_in = sb("x_in", [P, T, D])
        x_res = sb("x_res", [P, T, D])
        xn = sb("xn", [P, T, D])
        xn_res = sb("xn_res", [P, T, D])
        xt_st = sb("xt_st", [P, S])
        xt = sb("xt", [P, P])
        xs_hi = sb("xs_hi", [P, S], F32R)
        xs_lo = sb("xs_lo", [P, S], F32R)
        xt_hi = sb("xt_hi", [P, S], F32R)
        xt_lo = sb("xt_lo", [P, S], F32R)
        yq = sb("yq", [P, 2, S])
        yq_hi = sb("yq_hi", [P, 2, P], F32R)
        yq_lo = sb("yq_lo", [P, 2, P], F32R)
        v_sb = sb("v_sb", [P, T, H * E])
        prob = sb("prob", [P, 2, 2, 3 * P])
        nmax = sb("nmax", [P, 2, 4])
        den = sb("den", [P, 2, 4])
        rden = sb("rden", [P, 2, 4])
        pT0 = sb("pT0", [P, 2, S])
        pT1 = sb("pT1", [P, 2, P])
        hT = sb("hT", [P, S])
        shift = sb("shift", [P, 2, GT])
        x1 = sb("x1", [P, NT, D])
        att = sb("att", [P, T, D])
        z1 = sb("z1", [P, T, D])
        z2 = sb("z2", [P, T, D])
        z3 = sb("z3", [P, T, D])
        stat = {k: sb(f"stat_{k}", [P, GT, 6]) for k in ("x", "a", "z", "f", "o0", "o1")}
        mv = {k: sb(f"mv_{k}", [P, GT, 2]) for k in ("x", "a", "z", "f", "o0", "o1")}
        ve = {k: sb(f"ve_{k}", [P, GT]) for k in ("x", "a", "z", "f", "o0", "o1")}
        rstd = {k: sb(f"rstd_{k}", [P, GT]) for k in ("x", "a", "z", "f", "o0", "o1")}

        xf = sb("xf", [P, T, D])

        rec = [sb(f"rec{r}", [P, T, REC]) for r in range(K)]
        xfT = sb("xfT", [P, S])
        rmax = sb("rmax", [P, T])
        lg = sb("lg", [P, T, NE])
        ex = sb("ex", [P, T, NE])
        rsum = sb("rsum", [P, T])
        rrs = sb("rrs", [P, T])
        pr = sb("pr", [P, T, NE])
        top = sb("top", [P, T, 8])
        topi = sb("topi", [P, T, 8], U32)
        topf = sb("topf", [P, T, 8])
        sel = [sb(f"sel{r}", [P, T, NE]) for r in range(K)]
        sel_bf = sb("sel_bf", [P, T, NE], BF16)
        before = sb("before", [P, 2 * T * NE])
        place = sb("place", [P, T, NE])
        picked = sb("picked", [P, K, T, NE])
        slot_f = sb("slot_f", [P, K, T])
        slot = sb("slot", [P, K, T], I32)
        iota_e = sb("iota_e", [P, T, NE])
        ids = sb("ids", [P, K, T])
        base0 = sb("base0", [P, NE])
        base = sb("base", [P, NE])
        earlier = sb("earlier", [P, P], BF16)
        ones_bf = sb("ones_bf", [P, P], BF16)
        pad_rec = sb("pad_rec", [P, SPARE, REC])
        tile_no = sb("tile_no", [1, TILES])
        ones_row = sb("ones_row", [1, NE])
        cnt_f = sb("cnt_f", [1, NE])
        cnt_i = sb("cnt_i", [1, NE], I32)
        n_tiles = sb("n_tiles", [1, NE])
        ends = sb("ends", [1, NE])
        over = sb("over", [1, LATE, NE])
        over_n = sb("over_n", [1, LATE, NE])
        upto = sb("upto", [1, NE + 1])
        early = sb("early", [1, NE + 1])
        left = sb("left", [1, NE])
        skip = sb("skip", [1, NE])
        first_row = sb("first_row", [1, 1])
        tile_e = sb("tile_e", [1, LATE])
        tile_s = sb("tile_s", [1, LATE])
        tile_r = sb("tile_r", [1, LATE])
        expert_of = sb("expert_of", [1, TILES + RING], I32)
        row_of = sb("row_of", [1, TILES], I32)
        pad_row = sb("pad_row", [1, NE], I32)

        got = sb("got", [P, RING, REC])
        gT_hi = sb("gT_hi", [P, 2, P], F32R)
        gT_lo = sb("gT_lo", [P, 2, P], F32R)
        hid = sb("hid", [P, 2, F])
        hidT = sb("hidT", [P, 2, F])
        yo = v_sb[:].rearrange("p t c -> p (t c)")[:, 0:RING * D].rearrange("p (k d) -> p k d", k=RING)

        zz = w1_in[:].rearrange("p e f -> p (e f)").rearrange("p (s r k d) -> p s r k d", s=4, r=K, k=GT)
        zn = hid[:].rearrange("p s (k d) -> p s k d", k=GT)
        y_out = sb("y_out", [P, 2, GT, D])

        S1 = [bank("S1a"), bank("S1b")]
        S0, PT0, PT1, O, M, A = (bank(n) for n in ("S0", "PT0", "PT1", "O", "M", "A"))

        y_mm, y_sb = sem("y_mm"), sem("y_sb")
        s1_mm, s0_mm = sem("s1_mm"), sem("s0_mm")
        mx1, mx0, ex1, ex0 = sem("mx1"), sem("mx0"), sem("ex1"), sem("ex0")
        rc, nrm = sem("rc"), sem("nrm")
        t0_mm, t1_mm = sem("t0_mm"), sem("t1_mm")
        pt0_sb, pt1_sb = sem("pt0_sb"), sem("pt1_sb")
        pv_mm, o_sb = sem("pv_mm"), sem("o_sb")
        got_ld = [sem(f"got_ld{k}") for k in range(RING)]
        back_st = [sem(f"back_st{k}") for k in range(RING)]
        zz_ld = [sem(f"zz_ld{k}") for k in range(4)]
        out_st = [sem(f"out_st{k}") for k in range(2)]
        v_mm, v_done = sem("v_mm"), sem("v_done")
        y_h, y_lo = sem("y_h"), sem("y_lo")
        wq_ld = [sem(f"wq_ld{g}") for g in range(2)]
        wk_ld = [sem(f"wk_ld{g}") for g in range(2)]

        block = ctx.enter_context(nc.Block())

        up_bank, out_bank, rows_bank = (S1[0], S1[1]), (O, A), S0
        sum_bank = (S1[0], S1[1], S0, PT0)

        m_banks = ((PT1, O), (A, PT0))

        def m_part(m, g, i):
            return m[:, 8 * g + i:8 * g + 8:2, :]

        LAG = 2

        def over_batches(body):
            def run(eng):
                for b in range(LAG + 1):
                    body(b)
                with eng.Fori(LAG + 1, B - 1) as b:
                    body(b)
                for b in range(B - 1, B + LAG):
                    body(b)
            return run

        def there(b, back=0):
            return not isinstance(b, int) or 0 <= b - back < B

        def is_last(b):
            return isinstance(b, int) and b == B - 1

        def at(b, n, size):
            return slice(b * n, b * n + size) if isinstance(b, int) else bass.ds(b * n, size)

        @block.sync
        def _(sp):
            sp.dma_start(x_in[:], x_tiles[0]).then_inc(sem("x_in_ld"), 16)
            for g in range(2):
                hs = slice(8 * g, 8 * g + 8)
                sp.dma_start(wq_in[:, hs, :], wq[hs].rearrange("h d e -> d h e")).then_inc(wq_ld[g], 16)
                sp.dma_start(wk_in[:, hs, :], wk[hs].rearrange("h d e -> d h e")).then_inc(wk_ld[g], 16)
            sp.dma_start(wv_in[:].rearrange("p (h e) -> p h e", h=H),
                         wv.rearrange("h d e -> d h e")).then_inc(sem("wv_ld"), 16)
            sp.dma_start(wo_sb[:], wo.rearrange("(c p) d -> p c d", p=P)).then_inc(sem("wo_ld"), 16)
            for t in range(T):
                sp.dma_start(gamma_t[:, t, :], gamma.rearrange("(a d) -> a d", a=1).broadcast_to([P, D]))\
                    .then_inc(sem("gb_ld"), 16)
                sp.dma_start(beta_t[:, t, :], beta.rearrange("(a d) -> a d", a=1).broadcast_to([P, D]))\
                    .then_inc(sem("gb_ld"), 16)
            sp.dma_start(rw_sb[:], router_w).then_inc(sem("ffn_ld"), 16)
            sp.dma_start(w1_in[:], w1.rearrange("e d f -> d e f")).then_inc(sem("w1_ld"), 16)
            for e in range(NE):
                sp.dma_start(w2_sb[:, e], w2[e].rearrange("(c p) d -> p c d", p=P)).then_inc(sem("ffn_ld"), 16)

            sp.wait_ge(sem("pad_ok"), 1)
            sp.dma_start(sent[NE * CAP:NE * CAP + (SPARE - NE) * P, :].rearrange("(k p) c -> p k c", p=P),
                         pad_rec[:, NE:, :]).then_inc(sem("spare_st"), 16)

            def batch(b):
                if there(b, -1) and there(b):
                    sp.wait_ge(sem("xn_done"), b + 1)
                    sp.dma_start(x_in[:], x_tiles[b + 1]).then_inc(sem("x_in_ld"), 16)
                if there(b, 1):
                    if there(b, 2):
                        sp.wait_ge(sem("x1_done"), b - 1)
                    sp.dma_start(x_res[:], x_tiles[b - 1]).then_inc(sem("x_res_ld"), 16)

            def table_values(row, largest, why):
                return nc.values_load_multi_w_load_instructions(
                    row, engines=[mybir.EngineType.SP], min_val=0, max_val=largest,
                    skip_runtime_bounds_check_because=why)[1]

            def load_tiles(it, first):
                rows = table_values(row_of[0:1, at(it, RING, RING)], NE * CAP + (SPARE - NE) * P,
                                    "a tile's rows are in its expert's region or the spare tiles after the last")
                for k in range(RING):
                    if not first:
                        sp.wait_ge(back_st[k], 16 * it)
                    sp.dma_start(got[:, k, :], sent[bass.ds(rows[k], P), :]).then_inc(got_ld[k], 16)

            def batch_and_early(b):
                if isinstance(b, int) and b == B:
                    sp.wait_ge(sem("early_ok"), 1)
                    sp.wait_ge(sem("sent_st"), 16 * K * T * (B - 3))
                    load_tiles(0, True)
                batch(b)

            over_batches(batch_and_early)(sp)
            load_tiles(1, False)
            load_tiles(2, False)

            sp.wait_ge(sem("pads_known"), 1)
            rows = table_values(pad_row[0:1, :], NE * CAP - P, "an expert gets N rows at most, its region has CAP")
            for e in range(NE // 2):
                sp.dma_start(sent[bass.ds(rows[e], P), :], pad_rec[:, e, :]).then_inc(sem("pad_st"), 16)
            sp.wait_ge(sem("sent_st"), 16 * K * NT)
            sp.wait_ge(sem("pad_st"), 16 * NE)
            sp.wait_ge(sem("spare_st"), 16)
            sp.wait_ge(sem("table_ok"), 1)
            with sp.Fori(EARLY // RING, TILES // RING) as it:
                load_tiles(it, False)

            for k in range(RING):
                sp.wait_ge(back_st[k], 16 * (TILES // RING))

            def load_results(g):
                for r in range(K):
                    sp.dma_start(zz[:, g % 4, r], back_groups[r, g]).then_inc(zz_ld[g % 4], 16)

            for g in range(4):
                load_results(g)
            for g in range(NG + 2):
                if g + 4 < NG:
                    sp.wait_ge(sem("z_sum"), g + 1)
                    load_results(g + 4)
                if g >= 2:
                    sp.wait_ge(sem("y_out_done"), g - 1)
                    sp.dma_start(out_groups[g - 2], y_out[:, g % 2]).then_inc(out_st[g % 2], 16)
            for k in range(2):
                sp.wait_ge(out_st[k], 16 * (NG // 2))

        @block.tensor
        def _(pe):
            mm = nc.tensor.matmul

            def x_transpose(b):
                pe.wait_ge(sem("xn_done"), b + 1)
                for t in range(T):
                    last = nc.tensor.transpose(M[:, t * P:(t + 1) * P], xn[:, t, :], ident[:])
                last.then_inc(sem("xt_mm"), 1)

            def w_transpose(g):
                for src, loaded, bk in ((wq_in, wq_ld[g], S1[g]), (wk_in, wk_ld[g], (S0, PT0)[g])):
                    pe.wait_ge(loaded, 16)
                    for c in range(4):
                        h = 8 * g + 2 * c
                        last = nc.tensor.transpose(bk[:, c * P:(c + 1) * P],
                                                   src[:, h:h + 2, :].rearrange("p h e -> p (h e)"), ident[:])
                    last.then_inc(sem("wT_mm"), 1)

            def m_products(g, hs):
                pe.wait_ge(sem("wqT_sb"), g + 1)
                pe.wait_ge(sem("wkT_sb"), g + 1)
                for h in hs:
                    r = E * (h % 2)
                    last = mm(m_banks[g][h % 2][:, (h % 8 // 2) * P:(h % 8 // 2 + 1) * P],
                              wqT[r:r + E, h // 2, :], wkT[r:r + E, h // 2, :], start=True, stop=True)
                if h % 8 == 7:
                    last.then_inc(sem("m_mm"), 1)

            pe.wait_ge(sem("ident_ok"), 1)
            w_transpose(0)
            x_transpose(0)
            m_products(0, range(8))
            w_transpose(1)

            def product3(dst, a_hi, a_lo, b_hi, b_lo, start=True):
                mm(dst, a_hi, b_hi, start=start, stop=False, skip_group_check=True)
                mm(dst, a_hi, b_lo, start=False, stop=False, skip_group_check=True)
                return mm(dst, a_lo, b_hi, start=False, stop=True, skip_group_check=True)

            def y_proj(c):
                for k in range(2):
                    h = 2 * c + k
                    last = product3(M[:, k * S:(k + 1) * S], m_hi[:, h, :], m_lo[:, h, :],
                                    xt_hi[:], xt_lo[:], start=(k == 0))
                last.then_inc(y_mm, 1)

            def v_proj(t, half_of_heads):
                cols = slice(half_of_heads * 512, half_of_heads * 512 + 512)
                ts = slice(t * P, (t + 1) * P)
                product3(M[:, :], xt_hi[:, ts], xt_lo[:, ts], wv_hi[:, cols], wv_lo[:, cols]).then_inc(v_mm, 1)

            def scores(c):
                bk = S1[c % 2]
                for k in range(2):
                    product3(bk[:, k * S:(k + 1) * S], yq_hi[:, k, :], yq_lo[:, k, :], xs_hi[:], xs_lo[:],
                             start=(k == 0))
                for k in range(2):
                    last = mm(bk[:, k * S + P:(k + 1) * S], ident_bf[:], mask[:], start=False, stop=True,
                              skip_group_check=True)
                last.then_inc(s1_mm, 1)

            def scores0():
                for k in range(2):
                    mm(S0[:, k * P:(k + 1) * P], yq[:, k, 0:P], xt[:], start=(k == 0), stop=False,
                       skip_group_check=True)
                for k in range(2):
                    last = mm(S0[:, k * P:(k + 1) * P], ident_bf[:], mask[:], start=False, stop=True,
                              skip_group_check=True)
                last.then_inc(s0_mm, 1)

            def pv(c):
                for t, src, cols in ((0, pT0, slice(0, S)), (1, pT1, slice(P, S))):
                    for k in range(2):
                        h = 2 * c + k
                        last = mm(O[k * E:(k + 1) * E, cols], v_sb[:, t, h * E:(h + 1) * E], src[:, k, :],
                                  start=(t == 0), stop=(t == 1), skip_group_check=True)
                last.then_inc(pv_mm, 1)

            def w_o(c):
                for t in range(T):
                    last = mm(A[:, t * D:(t + 1) * D], hT[:, t * P:(t + 1) * P], wo_sb[:, c, :],
                              start=(c == 0 and t == 0), stop=(c == NP - 1), skip_group_check=True)
                if c == NP - 1:
                    last.then_inc(sem("wo_mm"), 1)

            def p_transpose(par):
                for k in range(2):
                    nc.tensor.transpose(PT0[:, k * S:k * S + P], prob[:, par, k, 0:P], ident[:])
                    last = nc.tensor.transpose(PT0[:, k * S + P:(k + 1) * S], prob[:, par, k, P:2 * P], ident[:])
                last.then_inc(t0_mm, 1)
                for k in range(2):
                    last = nc.tensor.transpose(PT1[:, k * P:(k + 1) * P], prob[:, par, k, 2 * P:3 * P], ident[:])
                last.then_inc(t1_mm, 1)

            pe.wait_ge(sem("xt_st"), 1)
            pe.wait_ge(sem("xt_split"), 1)
            pe.wait_ge(sem("m_split"), 2)
            y_proj(0)
            m_products(1, range(8, 12))
            pe.wait_ge(sem("wv_ok"), 1)
            pe.wait_ge(y_sb, 1)
            v_proj(0, 0)
            pe.wait_ge(sem("xt_ok"), 1)
            pe.wait_ge(sem("mask_ok"), 1)
            scores0()
            pe.wait_ge(y_lo, 1)
            pe.wait_ge(sem("xs_ok"), 1)
            scores(0)
            pe.wait_ge(v_done, 1)
            v_proj(1, 0)
            m_products(1, range(12, 16))
            pe.wait_ge(v_done, 2)
            y_proj(1)
            pe.wait_ge(sem("wo_ld"), 16)
            pe.wait_ge(sem("m_split"), 4)

            def batch(b):
                for j in range(NP):
                    p = NP * b + j
                    first = isinstance(b, int) and b == 0
                    nxt = there(b) if j < NP - 1 else there(b, -1)
                    nxt2 = there(b) if j < NP - 2 else there(b, -1)
                    last1 = there(b, 1) if j < 1 else there(b)
                    last2 = there(b, 1) if j < 2 else there(b)
                    if nxt and there(b):
                        pe.wait_ge(y_sb, p + 2)
                        if j == NP - 1:
                            pe.wait_ge(sem("xt_ok"), b + 2)
                        pe.wait_ge(ex0, p + 1)
                        scores0()
                        pe.wait_ge(y_lo, p + 2)
                        if j == NP - 1:
                            pe.wait_ge(sem("xs_ok"), b + 2)
                        if not (first and j == 0):
                            pe.wait_ge(ex1, p)
                        scores((j + 1) % 2)
                    if nxt2 and there(b):
                        if j in (0, 1, 2, 7) and not (first and j == 0):
                            pe.wait_ge(v_done, 4 * b + (5 if j == 7 else j + 2))
                        if j == 5 and there(b, -1):
                            pe.wait_ge(sem("xt_st"), b + 2)
                        if j == 6:
                            pe.wait_ge(sem("xt_split"), b + 2)
                        if there(b, 2):
                            if j == 3:
                                pe.wait_ge(sem("xfT_sb"), b - 1)
                            if j == 4:
                                pe.wait_ge(sem("lg_done"), b - 1)
                        y_proj((j + 2) % NP)
                    if last2:
                        pe.wait_ge(o_sb, p - 1)
                        if j == 2 and not first:
                            pe.wait_ge(sem("att_done"), b)
                        w_o((j - 2) % NP)
                    if last1:
                        pe.wait_ge(pt0_sb, p)
                        pe.wait_ge(pt1_sb, p)
                        if not (first and j == 1):
                            pe.wait_ge(o_sb, p - 1)
                        if j == 1:
                            pe.wait_ge(v_done, 4 * b + 2)
                        if j == 5:
                            pe.wait_ge(v_done, 4 * b + 4)
                        pv((j - 1) % NP)
                    extra = there(b) and (j in (0, 1) or (j in (4, 6, 7) and there(b, -1)))
                    router = there(b, 2) and j in (2, 3)
                    if (extra or router) and nxt2 and there(b):
                        pe.wait_ge(y_sb, p + 3)
                    if extra:
                        if j in (0, 1):
                            v_proj(j, 1)
                        elif j == 4:
                            x_transpose(b + 1)
                        else:
                            v_proj(j - 6, 0)
                    if router and j == 2:
                        pe.wait_ge(sem("xf_done"), b - 1)
                        for t in range(T):
                            last = nc.tensor.transpose(M[:, t * P:(t + 1) * P], xf[:, t, :], ident[:])
                        last.then_inc(sem("xfT_mm"), 1)
                    if router and j == 3:
                        pe.wait_ge(sem("xfT_sb"), b - 1)
                        for t in range(T):
                            last = mm(M[:, t * NE:(t + 1) * NE], xfT[:, t * P:(t + 1) * P], rw_sb[:],
                                      start=(t == 0), stop=True, skip_group_check=True)
                        last.then_inc(sem("logit_mm"), 1)
                    if there(b):
                        pe.wait_ge(nrm, p + 1)
                        if not (first and j == 0):
                            pe.wait_ge(pt0_sb, p)
                            pe.wait_ge(pt1_sb, p)
                    if there(b, 2) and j == 6:
                        if not there(b):
                            pe.wait_ge(pt1_sb, NP * B)
                            pe.wait_ge(sem("before_sb"), b - 2)
                        rows_before(b - 2)
                    if there(b):
                        p_transpose(j % 2)
                    if is_last(b) and j == NP - 1:
                        begin_tiles()
                    if not there(b):
                        epilogue_tile(b, j)

            def rows_before(r):
                pe.wait_ge(sem("sel_ok"), r + 1)
                c = 2 * P
                groups = [(0, [(earlier, 0)]), (1, [(earlier, 1), (ones_bf, 0)]), (2, [(ones_bf, 0), (ones_bf, 1)])]
                for g, terms in groups:
                    for n, (lhs, t) in enumerate(terms):
                        last = mm(PT1[:, c + g * NE:c + (g + 1) * NE], lhs[:], sel_bf[:, t, :],
                                  start=(g == 0), stop=(n == len(terms) - 1), skip_group_check=True)
                last.then_inc(sem("before_mm"), 1)

            w1h = w1_hi[:].rearrange("p e f -> p (e f)")
            w1l = w1_lo[:].rearrange("p e f -> p (e f)")
            w2f = w2_sb[:].rearrange("p e c d -> p (e c d)")
            assert F == NF * D

            def experts(first, n):
                return list(nc.values_load_multi_w_load_instructions(
                    expert_of[0:1, at(first, 1, n)], engines=[mybir.EngineType.PE], min_val=0,
                    max_val=(NE - 1) * F,
                    skip_runtime_bounds_check_because="the table's entries are clamped to the last expert")[1])

            def rows_T(n, k, it, first):
                pe.wait_ge(got_ld[k], 16 * (it + 1))
                if not first:
                    pe.wait_ge(sem("g_split"), n)
                nc.tensor.transpose(rows_bank[:, 0:P], got[:, k, 0:D], ident[:]).then_inc(sem("gT_mm"), 1)

            def up(n, k, e, first):
                pe.wait_ge(sem("g_split"), n + 1)
                if not first:
                    pe.wait_ge(sem("gelu"), n - 1)
                c = bass.ds(e, F)
                product3(up_bank[k % 2][:, :], gT_hi[:, k % 2, :], gT_lo[:, k % 2, :], w1h[:, c], w1l[:, c])\
                    .then_inc(sem("up_mm"), 1)

            def hidden_T(n, k, first):
                pe.wait_ge(sem("gelu"), n + 1)
                if not first:
                    pe.wait_ge(sem("hidT_sb"), n)
                for c in range(NF):
                    last = nc.tensor.transpose(PT0[:, c * P:(c + 1) * P], hid[:, k % 2, c * P:(c + 1) * P], ident[:])
                last.then_inc(sem("hidT_mm"), 1)

            def down(n, k, e, first):
                pe.wait_ge(sem("hidT_sb"), n + 1)
                if first:
                    pe.wait_ge(sem("att_done"), B)
                else:
                    pe.wait_ge(sem("yo_done"), n - 1)
                w2_e = w2f[:, bass.ds(e, F)]
                for c in range(NF):
                    last = mm(out_bank[k % 2][:, 0:D], hidT[:, k % 2, c * P:(c + 1) * P],
                              w2_e[:, c * D:(c + 1) * D], start=(c == 0), stop=(c == NF - 1))
                last.then_inc(sem("out_mm"), 1)

            def tile_step(it, k, e):
                n = it * RING + k
                first, last = isinstance(n, int) and n == 0, isinstance(n, int) and n == TILES - 1
                hidden_T(n, k, first)
                if not last:
                    up(n + 1, (k + 1) % RING, e[k + 2], first)
                if not (isinstance(n, int) and n + 2 >= TILES):
                    rows_T(n + 2, (k + 2) % RING, it + (k + 2) // RING, False)
                if not first:
                    down(n - 1, (k - 1) % RING, e[k], isinstance(n, int) and n <= 2)
                if last:
                    down(n, k, e[k + 1], False)

            def ring(it):
                e = experts(it * RING, RING + 2)
                for k in range(RING):
                    tile_step(it, k, e)

            offsets = []

            def begin_tiles():
                pe.wait_ge(sem("w1_ok"), 1)
                pe.wait_ge(sem("ffn_ld"), 16 * (NE + 1))
                pe.wait_ge(sem("early_ok"), 1)
                pe.wait_ge(ex0, NP * B)
                rows_T(0, 0, 0, True)
                rows_T(1, 1, 0, False)
                pe.wait_ge(ex1, NP * B)
                up(0, 0, experts(0, 2)[1], True)

            def epilogue_tile(b, j):
                if j == 0:
                    offsets[:] = experts((b - B) * RING, RING + 2)
                tile_step(b - B, j, offsets)

            over_batches(batch)(pe)

            e = experts(EARLY - RING, RING + 1)
            for k in range(RING):
                if k == RING - 1:
                    pe.wait_ge(sem("table_ok"), 1)
                    e += experts(EARLY + 1, 1)
                tile_step(EARLY // RING - 1, k, e)
            with pe.Fori(EARLY // RING, TILES // RING - 1) as it:
                ring(it)
            ring(TILES // RING - 1)

            for g in range(NG):
                pe.wait_ge(zz_ld[g % 4], 16 * K * (g // 4 + 1))
                if g >= 4:
                    pe.wait_ge(sem("zn_done"), g - 3)
                for r in range(K):
                    last = mm(sum_bank[g % 4][:], ident[:], zz[:, g % 4, r].rearrange("p t d -> p (t d)"),
                              start=(r == 0), stop=(r == K - 1))
                last.then_inc(sem("z_sum"), 1)

        @block.vector
        def _(dve):
            v = nc.vector

            def moments(kind, tiles):
                for t in range(tiles):
                    last = v.bn_aggr(mv[kind][:, t, :], stat[kind][:, t, :])
                return last

            def normalise(kind, dst, src, tiles):
                for t in range(tiles):
                    last = v.tensor_scalar(dst[:, t, :], src[:, t, :], mv[kind][:, t, 0:1], rstd[kind][:, t:t + 1],
                                           ALU.subtract, ALU.mult)
                return last

            def layer_stats(kind, src, tiles):
                for t in range(tiles):
                    v.bn_stats(stat[kind][:, t, :], src[:, t, :])
                dve.drain()
                moments(kind, tiles).then_inc(sem(f"mv_{kind}"), 1)

            dve.wait_ge(sem("x_in_ld"), 16)
            layer_stats("x", x_in, T)

            def xs_copy():
                v.tensor_copy(xt[:], xt_st[:, 0:P])
                v.tensor_copy(xs_lo[:], xt_lo[:].bitcast(F32)).then_inc(sem("xt_ok"), 1)

            def x_split(b):
                dve.wait_ge(sem("xt_st"), b + 1)
                v.tensor_copy(xt_hi[:], xt_st[:]).then_inc(sem("xt_h"), 1)
                dve.wait_ge(sem("xt_h"), b + 1)
                v.tensor_tensor(xt_lo[:], xt_st[:], xt_hi[:].bitcast(F32), ALU.subtract).then_inc(sem("xt_split"), 1)

            def y_low(p):
                dve.wait_ge(y_h, p + 1)
                v.tensor_tensor(yq_lo[:], yq[:, :, P:S], yq_hi[:].bitcast(F32), ALU.subtract).then_inc(y_lo, 1)

            def maxima0(p, par):
                dve.wait_ge(s0_mm, p + 1)
                v.tensor_reduce(nmax[:, par, 2:4], S0[:, 0:2 * P].rearrange("p (k t) -> p k t", k=2), AX_X, ALU.max,
                                negate=True).then_inc(mx0, 1)

            def maxima1(p, par):
                dve.wait_ge(s1_mm, p + 1)
                v.tensor_reduce(nmax[:, par, 0:2], S1[par][:].rearrange("p (k t) -> p k t", k=2), AX_X, ALU.max,
                                negate=True).then_inc(mx1, 1)

            def wk_copy(g):
                dve.wait_ge(sem("wT_mm"), 2 * g + 2)
                v.tensor_copy(wkT[:, 4 * g:4 * g + 4, :], (S0, PT0)[g][:].rearrange("p (c d) -> p c d", c=4))\
                    .then_inc(sem("wkT_sb"), 1)

            def m_low(g):
                for i in range(2):
                    dve.wait_ge(sem("m_h"), 2 * g + i + 1)
                    v.scalar_tensor_tensor(m_part(m_lo, g, i), m_banks[g][i][:].rearrange("p (c d) -> p c d", c=4),
                                           float(E) ** -0.5, m_part(m_hi, g, i).bitcast(F32), ALU.mult,
                                           ALU.subtract).then_inc(sem("m_split"), 1)

            dve.wait_ge(sem("rstd_x"), 1)
            normalise("x", xn, x_in, T).then_inc(sem("xn_done"), 1)
            wk_copy(0)
            x_split(0)
            dve.wait_ge(sem("xt_split"), 1)
            xs_copy()
            m_low(0)
            wk_copy(1)
            dve.wait_ge(sem("wv_ld"), 16)
            v.tensor_copy(wv_hi[:], wv_in[:]).then_inc(sem("wv_h"), 1)
            dve.wait_ge(sem("wv_h"), 1)
            v.tensor_tensor(wv_lo[:], wv_in[:], wv_hi[:].bitcast(F32), ALU.subtract).then_inc(sem("wv_ok"), 1)
            y_low(0)
            maxima0(0, 0)
            maxima1(0, 0)
            m_low(1)
            y_low(1)

            def batch(b):
                for j in range(NP):
                    p = NP * b + j
                    par = j % 2
                    if there(b):
                        dve.wait_ge(ex1, p + 1)
                        v.reciprocal(rden[:, par, :], den[:, par, :]).then_inc(rc, 1)
                        if j < NP - 1 or there(b, -1):
                            maxima0(p + 1, (j + 1) % 2)
                        dve.wait_ge(rc, p + 1)
                        for k in range(2):
                            v.tensor_scalar(prob[:, par, k, P:3 * P], prob[:, par, k, P:3 * P],
                                            rden[:, par, k:k + 1], None, ALU.mult)
                            q = v.tensor_scalar(prob[:, par, k, 0:P], prob[:, par, k, 0:P],
                                                rden[:, par, 2 + k:3 + k], None, ALU.mult)
                        q.then_inc(nrm, 1)
                        if j < NP - 1 or there(b, -1):
                            maxima1(p + 1, (j + 1) % 2)
                    if there(b) and (j < NP - 2 or there(b, -1)):
                        y_low(p + 2)
                    if there(b, 1):
                        if there(b):
                            tail(b - 1, j)
                        elif j != 6:
                            tail(b - 1, 6 if j == 5 else j)
                    if there(b) and there(b, -1):
                        ahead(b + 1, j)
                    if isinstance(b, int) and b == B and j == 5:
                        router(B - 1, 0)
                    if there(b, 2) and not (isinstance(b, int) and b == B + 1 and j == 0):
                        router(b - 2, j)
                    if there(b, 2) and j == NP - 1:
                        dispatch(b - 2)
                    if there(b, 2) and j == 6:
                        if there(b):
                            dve.wait_ge(t1_mm, p + 1)
                        dve.wait_ge(sem("before_mm"), b - 1)
                        v.tensor_copy(before[:, 0:(T + 1) * NE], PT1[:, 2 * P:2 * P + (T + 1) * NE])\
                            .then_inc(sem("before_sb"), 1)
                    if there(b):
                        dve.wait_ge(t1_mm, p + 1)
                        v.tensor_copy(pT1[:], PT1[:, 0:2 * P].rearrange("p (k s) -> p k s", k=2)).then_inc(pt1_sb, 1)
                    if is_last(b) and j < NP - 1:
                        early_table(j)
                    if is_last(b) and j == NP - 1:
                        begin_tiles()
                    if not there(b):
                        if b == B + 1 and j == NP - 1:
                            late_table(0)
                        tile_step((b - B) * RING + j, j)

            def over_e(a):
                return a.unsqueeze(2).broadcast_to([P, T, NE])

            def router(r, j):
                if j == 0:
                    rows = x1[:, at(r, T, T), :]
                    dve.wait_ge(sem("x1_done"), r + 1)
                    for t in range(T):
                        v.bn_stats(stat["f"][:, t, :], rows[:, t, :])
                    dve.drain()
                    moments("f", T).then_inc(sem("mv_f"), 1)
                if j == 1:
                    rows = x1[:, at(r, T, T), :]
                    dve.wait_ge(sem("rstd_f"), r + 1)
                    if not (isinstance(r, int) and r == 0):
                        dve.wait_ge(sem("rec_ok"), r)
                    for t in range(T):
                        q = v.tensor_scalar(xf[:, t, :], rows[:, t, :], mv["f"][:, t, 0:1],
                                            rstd["f"][:, t:t + 1], ALU.subtract, ALU.mult)
                    q.then_inc(sem("xf_done"), 1)
                if j == 3:
                    logits = M[:, 0:T * NE].rearrange("p (t e) -> p t e", t=T)
                    dve.wait_ge(sem("logit_mm"), r + 1)
                    v.tensor_reduce(rmax[:], logits, AX_X, ALU.max)
                    dve.drain()
                    v.tensor_tensor(lg[:], logits, over_e(rmax[:]), ALU.subtract).then_inc(sem("lg_done"), 1)
                if j == 4:
                    dve.wait_ge(sem("rexp"), r + 1)
                    v.tensor_reduce(rsum[:], ex[:], AX_X, ALU.add)
                    dve.drain()
                    v.reciprocal(rrs[:], rsum[:])
                    dve.drain()
                    v.tensor_tensor(pr[:], ex[:], over_e(rrs[:]), ALU.mult)
                    dve.drain()
                    for t in range(T):
                        v.max(top[:, t, :], pr[:, t, :])
                    dve.drain()
                    for t in range(T):
                        v.max_index(topi[:, t, :], top[:, t, :], pr[:, t, :])
                if j == 5:
                    dve.drain()
                    v.tensor_copy(topf[:], topi[:])
                    dve.drain()
                    for k in range(K):
                        v.tensor_tensor(sel[k][:], iota_e[:], over_e(topf[:, :, k]), ALU.is_equal)
                    dve.drain()
                    v.tensor_tensor(sel_bf[:], sel[0][:], sel[1][:], ALU.add).then_inc(sem("sel_ok"), 1)
                if j == 6:
                    if not (isinstance(r, int) and r == 0):
                        dve.wait_ge(sem("sent_st"), 16 * K * T * r)
                    for k in range(K):
                        v.tensor_copy(rec[k][:, :, C_GATE], top[:, :, k])
                        v.tensor_copy(rec[k][:, :, C_ID].bitcast(I32), ids[:, k, :])

            def dispatch(r):
                dve.drain()
                v.tensor_scalar(ids[:], ids[:], float(S), None, ALU.add)
                v.tensor_tensor(place[:], before[:, 0:T * NE].rearrange("p (t e) -> p t e", t=T),
                                base[:].unsqueeze(1).broadcast_to([P, T, NE]), ALU.add)
                dve.drain()
                v.tensor_tensor(base[:], base[:], before[:, T * NE:(T + 1) * NE], ALU.add)
                for k in range(K):
                    v.tensor_tensor(picked[:, k], place[:], sel[k][:], ALU.mult)
                dve.drain()
                v.tensor_reduce(slot_f[:], picked[:], AX_X, ALU.add)
                dve.drain()
                v.tensor_copy(slot[:], slot_f[:]).then_inc(sem("slot_ok"), 1)

            def ahead(b, j):
                if j == 0:
                    dve.wait_ge(sem("x_in_ld"), 16 * b + 16)
                    layer_stats("x", x_in, T)
                if j == 2:
                    dve.wait_ge(sem("rstd_x"), b + 1)
                    dve.wait_ge(sem("xn_kept"), b)
                    normalise("x", xn, x_in, T).then_inc(sem("xn_done"), 1)
                if j == 5:
                    dve.wait_ge(y_mm, NP * b)
                    x_split(b)
                if j == 6:
                    xs_copy()

            def tail(b, j):
                if j == 1:
                    dve.wait_ge(sem("wo_mm"), b + 1)
                    v.tensor_tensor(att[:], xn_res[:], A[:, 0:T * D].rearrange("p (t d) -> p t d", t=T), ALU.add)\
                        .then_inc(sem("att_done"), 1)
                    dve.wait_ge(sem("att_done"), b + 1)
                    layer_stats("a", att, T)
                if j == 2:
                    dve.wait_ge(sem("rstd_a"), b + 1)
                    normalise("a", z1, att, T).then_inc(sem("z1_done"), 1)
                    if is_last(b):
                        dve.drain()
                        v.tensor_tensor(z2[:], z1[:], gamma_t[:], ALU.mult)
                        dve.drain()
                        v.tensor_tensor(z2[:], z2[:], beta_t[:], ALU.add).then_inc(sem("z2_done"), 1)
                if j == 3:
                    dve.wait_ge(sem("z2_done"), b + 1)
                    layer_stats("z", z2, T)
                if j == 6:
                    dve.wait_ge(sem("rstd_z"), b + 1)
                    normalise("z", z3, z2, T).then_inc(sem("z3_done"), 1)
                    if is_last(b):
                        dve.drain()
                        dve.wait_ge(sem("x_res_ld"), 16 * B)
                        v.tensor_tensor(x1[:, at(b, T, T), :], x_res[:], z3[:], ALU.add).then_inc(sem("x1_done"), 1)

            dve.wait_ge(sem("consts_ok"), 1)
            v.tensor_copy(base[:], base0[:])

            def count_tiles(round_up):
                v.tensor_tensor(cnt_f[:], base[0:1, :], base0[0:1, :], ALU.subtract)
                dve.drain()
                v.tensor_scalar(cnt_i[:], cnt_f[:], float(round_up), None, ALU.add)

            def to_float():
                v.tensor_scalar(cnt_i[:], cnt_i[:], P.bit_length() - 1, None, ALU.logical_shift_right)
                dve.drain()
                v.tensor_copy(n_tiles[:], cnt_i[:])

            def spans(n, per_expert):
                v.tensor_tensor_scan(ends[:], ones_row[:], per_expert[:], 0.0, ALU.mult, ALU.add)
                dve.drain()
                v.tensor_tensor(over[:, 0:n], ends[:].unsqueeze(1).broadcast_to([1, n, NE]),
                                tile_no[:, 0:n].unsqueeze(2).broadcast_to([1, n, NE]), ALU.is_le)

            def skips(n):
                v.tensor_tensor(over_n[:, 0:n], over[:, 0:n], skip[:].unsqueeze(1).broadcast_to([1, n, NE]), ALU.mult)
                v.tensor_reduce(tile_e[:, 0:n], over[:, 0:n], AX_X, ALU.add)

            def offsets(first, n):
                v.tensor_reduce(tile_s[:, 0:n], over_n[:, 0:n], AX_X, ALU.add)
                v.tensor_scalar(expert_of[:, first + 1:first + 1 + n], tile_e[:, 0:n], float(NE - 1), float(F),
                                ALU.min, ALU.mult)

            def early_table(j):
                dve.drain()
                if j == 0:
                    v.memset(expert_of[:], 0)
                    v.memset(upto[:], 0.0)
                    v.memset(early[:], 0.0)
                    count_tiles(0)
                if j == 1:
                    to_float()
                if j == 2:
                    spans(EARLY, n_tiles)
                if j == 3:
                    v.tensor_scalar(upto[:, 1:NE + 1], ends[:], float(EARLY), None, ALU.min)
                    v.tensor_scalar(skip[:], n_tiles[:], -float(P), float(CAP), ALU.mult, ALU.add)
                    dve.drain()
                    v.tensor_tensor(early[:, 0:NE], upto[:, 1:NE + 1], upto[:, 0:NE], ALU.subtract)
                    skips(EARLY)
                if j == 4:
                    offsets(0, EARLY)
                if j == 5:
                    v.scalar_tensor_tensor(tile_r[:, 0:EARLY], tile_no[:, 0:EARLY], float(P), tile_s[:, 0:EARLY],
                                           ALU.mult, ALU.add)
                    v.tensor_scalar(first_row[:], early[:, 0:1], float(P), None, ALU.mult)
                    dve.drain()
                    v.tensor_copy(row_of[:, 0:EARLY], tile_r[:, 0:EARLY]).then_inc(sem("early_ok"), 1)

            def late_table(step):
                if step > 5:
                    return
                dve.drain()
                if step == 0:
                    v.tensor_copy(pad_row[:], base[0:1, :]).then_inc(sem("pads_known"), 1)
                    count_tiles(P - 1)
                if step == 1:
                    to_float()
                    dve.drain()
                    v.tensor_tensor(left[:], n_tiles[:], early[:, 0:NE], ALU.subtract)
                if step == 2:
                    spans(LATE, left)
                    v.tensor_tensor(skip[:], early[:, 1:NE + 1], early[:, 0:NE], ALU.subtract)
                if step == 3:
                    v.tensor_tensor(skip[:], skip[:], left[:], ALU.subtract)
                    dve.drain()
                    v.tensor_scalar(skip[:], skip[:], float(P), float(CAP), ALU.mult, ALU.add)
                    dve.drain()
                    skips(LATE)
                if step == 4:
                    offsets(EARLY, LATE)
                if step == 5:
                    v.scalar_tensor_tensor(tile_r[:], tile_no[:, 0:LATE], float(P), tile_s[:], ALU.mult, ALU.add)
                    dve.drain()
                    v.tensor_scalar(row_of[:, EARLY:TILES], tile_r[:], first_row[:], None, ALU.add)\
                        .then_inc(sem("table_ok"), 1)

            def split_rows(n, k):
                dve.wait_ge(sem("gT_mm"), n + 1)
                v.tensor_copy(gT_hi[:, k % 2, :], rows_bank[:, 0:P]).then_inc(sem("g_h"), 1)
                dve.wait_ge(sem("g_h"), n + 1)
                v.tensor_tensor(gT_lo[:, k % 2, :], rows_bank[:, 0:P], gT_hi[:, k % 2, :].bitcast(F32),
                                ALU.subtract).then_inc(sem("g_split"), 1)

            def begin_tiles():
                split_rows(0, 0)
                split_rows(1, 1)

            def tile_step(n, k):
                dve.wait_ge(sem("hidT_mm"), n + 1)
                if not (isinstance(n, int) and n < 2):
                    dve.wait_ge(sem("out_mm"), n - 1)
                v.tensor_copy(hidT[:, k % 2, :], PT0[:]).then_inc(sem("hidT_sb"), 1)
                if not (isinstance(n, int) and n + 2 >= TILES):
                    if isinstance(n, int) and n == 0:
                        dve.wait_ge(sem("up_mm"), 1)
                    split_rows(n + 2, k)

            over_batches(batch)(dve)

            for k in range(RING):
                tile_step(EARLY - RING + k, k)
                late_table(k + 1)
            with dve.Fori(EARLY // RING, TILES // RING - 1) as it:
                for k in range(RING):
                    tile_step(it * RING + k, k)
            for k in range(RING):
                tile_step(TILES - RING + k, k)

            for g in range(NG + 2):
                if g < NG:
                    o = f"o{g % 2}"
                    dve.wait_ge(sem("z_sum"), g + 1)
                    for t in range(GT):
                        v.bn_stats(stat[o][:, t, :], sum_bank[g % 4][:, t * D:(t + 1) * D])
                    dve.drain()
                    if g >= 2:
                        dve.wait_ge(sem("zn_done"), g - 1)
                    for t in range(GT):
                        q = v.bn_aggr(mv[o][:, t, :], stat[o][:, t, :])
                    q.then_inc(sem("mv_o"), 1)
                if 1 <= g <= NG:
                    h = g - 1
                    o = f"o{h % 2}"
                    dve.wait_ge(sem("rstd_o"), h + 1)
                    v.scalar_tensor_tensor(shift[:, h % 2, :], mv[o][:, :, 0], -1.0, rstd[o][:], ALU.mult, ALU.mult)\
                        .then_inc(sem("shift_ok"), 1)
                if g >= 2:
                    h = g - 2
                    dve.wait_ge(sem("zn_done"), h + 1)
                    if h >= 2:
                        dve.wait_ge(out_st[h % 2], 16 * (h // 2))
                    v.tensor_tensor(y_out[:, h % 2], x1[:, h * GT:(h + 1) * GT, :], zn[:, h % 2], ALU.add)\
                        .then_inc(sem("y_out_done"), 1)

        @block.scalar
        def _(act):
            a = nc.scalar
            def xt_copy(b):
                act.wait_ge(sem("xt_mm"), b + 1)
                a.activation(xt_st[:], M[:, 0:S], ACT.Copy).then_inc(sem("xt_st"), 1)

            def y_copy(p):
                act.wait_ge(y_mm, p + 1)
                a.activation(yq[:], M[:].rearrange("p (k s) -> p k s", k=2), ACT.Copy).then_inc(y_sb, 1)
                act.wait_ge(y_sb, p + 1)
                a.activation(yq_hi[:], yq[:, :, P:S], ACT.Copy).then_inc(y_h, 1)

            def xs_copy(b):
                act.wait_ge(sem("xt_split"), b + 1)
                a.activation(xs_hi[:], xt_hi[:].bitcast(F32), ACT.Copy).then_inc(sem("xs_ok"), 1)

            def exps(p, par):
                act.wait_ge(mx0, p + 1)
                for k in range(2):
                    q = a.activation(prob[:, par, k, 0:P], S0[:, k * P:(k + 1) * P], ACT.Exp,
                                     bias=nmax[:, par, 2 + k:3 + k], accum_out=den[:, par, 2 + k:3 + k])
                q.then_inc(ex0, 1)
                act.wait_ge(mx1, p + 1)
                for k in range(2):
                    q = a.activation(prob[:, par, k, P:3 * P], S1[par][:, k * S:(k + 1) * S], ACT.Exp,
                                     bias=nmax[:, par, k:k + 1], accum_out=den[:, par, k:k + 1])
                q.then_inc(ex1, 1)

            def v_copy(n, t, half_of_heads):
                act.wait_ge(v_mm, n)
                a.activation(v_sb[:, t, half_of_heads * 512:half_of_heads * 512 + 512], M[:], ACT.Copy)\
                    .then_inc(v_done, 1)

            def o_copy(p):
                act.wait_ge(pv_mm, p + 1)
                a.activation(hT[:], O[:, 0:S], ACT.Copy).then_inc(o_sb, 1)

            def wq_copy(g):
                act.wait_ge(sem("wT_mm"), 2 * g + 1)
                a.activation(wqT[:, 4 * g:4 * g + 4, :], S1[g][:].rearrange("p (c d) -> p c d", c=4), ACT.Copy)\
                    .then_inc(sem("wqT_sb"), 1)

            def m_high(g):
                act.wait_ge(sem("m_mm"), g + 1)
                for i in range(2):
                    a.activation(m_part(m_hi, g, i), m_banks[g][i][:].rearrange("p (c d) -> p c d", c=4), ACT.Copy,
                                 scale=float(E) ** -0.5).then_inc(sem("m_h"), 1)

            wq_copy(0)
            xt_copy(0)
            xs_copy(0)
            m_high(0)
            wq_copy(1)
            y_copy(0)
            v_copy(1, 0, 0)
            exps(0, 0)
            v_copy(2, 1, 0)
            m_high(1)
            y_copy(1)

            def batch(b):
                for j in range(NP):
                    p = NP * b + j
                    first = isinstance(b, int) and b == 0
                    if there(b):
                        if j < NP - 2 or there(b, -1):
                            y_copy(p + 2)
                        if j < NP - 1 or there(b, -1):
                            if not (first and j == 0):
                                act.wait_ge(t1_mm, p)
                            exps(p + 1, (j + 1) % 2)
                        if j == 6 and there(b, -1):
                            xs_copy(b + 1)
                    if (there(b) and not (first and j == 0)) or (j == 0 and there(b, 1)):
                        o_copy(p - 1)
                    if there(b):
                        if there(b, -1) and j == 4:
                            act.wait_ge(sem("xt_ok"), b + 1)
                            xt_copy(b + 1)
                        if j in (0, 1):
                            v_copy(4 * b + 3 + j, j, 1)
                        if there(b, -1) and j in (6, 7):
                            v_copy(4 * b + j - 1, j - 6, 0)
                    if there(b, 2):
                        if j == 2:
                            act.wait_ge(sem("xfT_mm"), b - 1)
                            a.activation(xfT[:], M[:, 0:S], ACT.Copy).then_inc(sem("xfT_sb"), 1)
                        if j == 3:
                            act.wait_ge(sem("lg_done"), b - 1)
                            a.activation(ex[:], lg[:], ACT.Exp).then_inc(sem("rexp"), 1)
                        if j == 5:
                            if there(b, 3):
                                act.wait_ge(sem("sent_st"), 16 * K * T * (b - 2))
                            for k in range(K):
                                q = a.activation(rec[k][:, :, 0:D], xf[:], ACT.Copy)
                            q.then_inc(sem("rec_ok"), 1)
                    if there(b):
                        act.wait_ge(t0_mm, p + 1)
                        a.activation(pT0[:], PT0[:].rearrange("p (k s) -> p k s", k=2), ACT.Copy)\
                            .then_inc(pt0_sb, 1)
                    if is_last(b) and j == NP - 1:
                        gelu(0, 0, True)
                    if not there(b):
                        tile_step(b - B, j)

            def gelu(n, k, first):
                act.wait_ge(sem("up_mm"), n + 1)
                if not first:
                    act.wait_ge(sem("hidT_mm"), n - 1)
                a.activation(hid[:, k % 2, :], up_bank[k % 2][:], ACT.Gelu_apprx_tanh).then_inc(sem("gelu"), 1)

            def gated(n, k, it):
                act.wait_ge(sem("out_mm"), n + 1)
                if not (isinstance(it, int) and it == 0):
                    act.wait_ge(back_st[k], 16 * it)
                a.activation(yo[:, k, :], out_bank[k % 2][:, 0:D], ACT.Copy, scale=got[:, k, C_GATE:C_GATE + 1])\
                    .then_inc(sem("yo_done"), 1)

            def tile_step(it, k):
                n = it * RING + k
                if not (isinstance(n, int) and n == TILES - 1):
                    gelu(n + 1, (k + 1) % RING, isinstance(n, int) and n == 0)
                if not (isinstance(n, int) and n == 0):
                    gated(n - 1, (k - 1) % RING, it if k else it - 1)
                if isinstance(n, int) and n == TILES - 1:
                    gated(n, k, it)

            over_batches(batch)(act)

            act.wait_ge(sem("pads_known"), 1)
            rows = nc.values_load_multi_w_load_instructions(
                pad_row[0:1, :], engines=[mybir.EngineType.Activation], min_val=0, max_val=NE * CAP - P,
                skip_runtime_bounds_check_because="an expert gets N rows at most, its region has CAP")[1]
            for e in range(NE // 2, NE):
                nc.scalar.dma_start(sent[bass.ds(rows[e], P), :], pad_rec[:, e, :]).then_inc(sem("pad_st"), 16)

            for k in range(RING):
                tile_step(EARLY // RING - 1, k)
            with act.Fori(EARLY // RING, TILES // RING - 1) as it:
                for k in range(RING):
                    tile_step(it, k)
            for k in range(RING):
                tile_step(TILES // RING - 1, k)

            for g in range(NG):
                h = g % 2
                act.wait_ge(sem("shift_ok"), g + 1)
                if g >= 2:
                    act.wait_ge(sem("y_out_done"), g - 1)
                for t in range(GT):
                    last_op = a.activation(zn[:, h, t, :], sum_bank[g % 4][:, t * D:(t + 1) * D], ACT.Identity,
                                           bias=shift[:, h, t:t + 1], scale=rstd[f"o{h}"][:, t:t + 1])
                last_op.then_inc(sem("zn_done"), 1)

        @block.gpsimd
        def _(pool):
            q = nc.gpsimd
            q.memset(ident[:], 0.0)
            q.memset(half[:], -0.5)
            q.memset(ln_eps[:], LN_EPS)
            q.memset(att_eps[:], ATT_EPS)
            q.memset(mask[:], 0.0).then_inc(sem("p_set"), 1)
            pool.wait_ge(sem("p_set"), 1)
            q.affine_select(out=ident[:], in_=ident[:], compare_op=ALU.not_equal, fill=1.0, base=0,
                            pattern=[[-1, P]], channel_multiplier=1).then_inc(sem("ident_ok"), 1)
            pool.wait_ge(sem("ident_ok"), 1)
            q.tensor_copy(ident_bf[:], ident[:])
            q.affine_select(out=mask[:], in_=mask[:], compare_op=ALU.is_ge, fill=MASKED, base=0,
                            pattern=[[-1, P]], channel_multiplier=1).then_inc(sem("mask_ok"), 1)
            def inverse_root(kind, tiles, eps, n):
                pool.wait_ge(sem(f"mv_{kind}"), n)
                q.tensor_tensor(ve[kind][:, 0:tiles], mv[kind][:, 0:tiles, 1], eps[:, 0:tiles], ALU.add)\
                    .then_inc(sem(f"ve_{kind}"), 1)
                pool.wait_ge(sem(f"ve_{kind}"), n)
                q.tensor_tensor(rstd[kind][:, 0:tiles], ve[kind][:, 0:tiles], half[:, 0:tiles], ALU.pow)\
                    .then_inc(sem(f"rstd_{kind}"), 1)

            inverse_root("x", T, ln_eps, 1)
            q.memset(ones_bf[:], 1.0)
            q.memset(earlier[:], 1.0)
            q.memset(ones_row[:], 1.0)
            q.memset(pad_rec[:], 0.0)
            for r in rec:
                q.memset(r[:], 0.0)
            q.iota(iota_e[:], pattern=[[0, T], [1, NE]], base=0, channel_multiplier=0,
                   allow_small_or_imprecise_dtypes=True)
            q.iota(ids[:], pattern=[[N, K], [P, T]], base=0, channel_multiplier=1,
                   allow_small_or_imprecise_dtypes=True)
            q.iota(base0[:], pattern=[[CAP, NE]], base=0, channel_multiplier=0,
                   allow_small_or_imprecise_dtypes=True)
            q.iota(tile_no[:], pattern=[[1, TILES]], base=0, channel_multiplier=0,
                   allow_small_or_imprecise_dtypes=True).then_inc(sem("iota_ok"), 1)
            pool.wait_ge(sem("iota_ok"), 1)
            q.affine_select(out=earlier[:], in_=earlier[:], compare_op=ALU.is_gt, fill=0.0, base=0,
                            pattern=[[1, P]], channel_multiplier=-1).then_inc(sem("consts_ok"), 1)
            q.iota(pad_rec[:, :, C_ID].bitcast(I32), pattern=[[P, SPARE]], base=K * N, channel_multiplier=1)\
                .then_inc(sem("pad_ok"), 1)

            pool.wait_ge(sem("gb_ld"), 16 * 2 * T)
            pool.wait_ge(sem("xn_done"), 1)
            q.tensor_copy(xn_res[:], xn[:]).then_inc(sem("xn_kept"), 1)
            def tail(b):
                inverse_root("a", T, att_eps, b + 1)
                if not (isinstance(b, int) and b == B - 1):
                    q.tensor_copy(xn_res[:], xn[:]).then_inc(sem("xn_kept"), 1)
                if not is_last(b):
                    pool.wait_ge(sem("z1_done"), b + 1)
                    q.tensor_tensor(z2[:], z1[:], gamma_t[:], ALU.mult).then_inc(sem("z_g"), 1)
                    pool.wait_ge(sem("z_g"), b + 1)
                    q.tensor_tensor(z2[:], z2[:], beta_t[:], ALU.add).then_inc(sem("z2_done"), 1)

            def tail_end(b):
                inverse_root("z", T, ln_eps, b + 1)
                if not is_last(b):
                    pool.wait_ge(sem("z3_done"), b + 1)
                    pool.wait_ge(sem("x_res_ld"), 16 * b + 16)
                    q.tensor_tensor(x1[:, at(b, T, T), :], x_res[:], z3[:], ALU.add).then_inc(sem("x1_done"), 1)

            def send(r, choices=range(K)):
                pool.wait_ge(sem("slot_ok"), r + 1)
                pool.wait_ge(sem("rec_ok"), r + 1)
                q.sem_inc(sem("send_turn"), 1)
                for k in choices:
                    for t in range(T):
                        q.indirect_dma_start(sent, bass.IndirectOffsetOnAxis(ap=slot[:, k, t:t + 1], axis=0),
                                             rec[k][:, t, :], None).then_inc(sem("sent_st"), 16)

            def store(n, k):
                pool.wait_ge(sem("yo_done"), n + 1)
                q.sem_inc(sem("store_turn"), 1)
                q.indirect_dma_start(back, bass.IndirectOffsetOnAxis(ap=got[:, k, C_ID:C_ID + 1].bitcast(I32), axis=0),
                                     yo[:, k, :], None).then_inc(back_st[k], 16)

            def stores(first, n):
                for m in range(first, n):
                    store(m, m % RING)

            def batch(b):
                if there(b) and there(b, -1):
                    inverse_root("x", T, ln_eps, b + 2)
                if isinstance(b, int) and b == 0:
                    pool.wait_ge(sem("w1_ld"), 16)
                    q.tensor_copy(w1_hi[:], w1_in[:]).then_inc(sem("w1_h"), 1)
                    pool.wait_ge(sem("w1_h"), 1)
                    q.tensor_tensor(w1_lo[:], w1_in[:], w1_hi[:].bitcast(F32), ALU.subtract).then_inc(sem("w1_ok"), 1)
                if there(b, 2) and there(b, 1):
                    inverse_root("f", T, ln_eps, b - 1)
                if there(b) and there(b, 1):
                    tail(b - 1)
                    tail_end(b - 1)
                if isinstance(b, int) and b == B:
                    send(B - 3, [0])
                    tail(B - 1)
                    stores(0, 1)
                    send(B - 3, [1])
                    tail_end(B - 1)
                    stores(1, 4)
                    inverse_root("f", T, ln_eps, B)
                    stores(4, 7)
                elif isinstance(b, int) and b == B + 1:
                    stores(7, 8)
                    send(B - 2, [0])
                    stores(8, 10)
                    send(B - 2, [1])
                    stores(10, 14)
                    send(B - 1)
                elif there(b, 2) and not is_last(b):
                    send(b - 2)

            over_batches(batch)(pool)

            stores(14, 2 * RING)
            with pool.Fori(2, TILES // RING) as it:
                for k in range(RING):
                    store(it * RING + k, k)

            for g in range(NG):
                o = f"o{g % 2}"
                pool.wait_ge(sem("mv_o"), g + 1)
                q.tensor_tensor(ve[o][:], mv[o][:, :, 1], ln_eps[:], ALU.add).then_inc(sem("ve_o"), 1)
                pool.wait_ge(sem("ve_o"), g + 1)
                q.tensor_tensor(rstd[o][:], ve[o][:], half[:], ALU.pow).then_inc(sem("rstd_o"), 1)



_INS = ["L0_attn_x", "L0_attn_Wq", "L0_attn_Wk", "L0_attn_Wv", "L0_attn_Wo", "L0_attn_gamma", "L0_attn_beta",
        "L0_ffn_router_w", "L0_ffn_w1", "L0_ffn_w2"]


def kernel(**inputs):
    import numpy as np
    import concourse.bacc as bacc
    from concourse.bass_utils import run_bass_kernel_spmd

    nc = bacc.Bacc("TRN2", target_bir_lowering=False, num_devices=1)
    arrays, args = {}, []
    for name in _INS:
        a = np.ascontiguousarray(inputs[name])
        arrays[name] = a
        args.append(nc.dram_tensor(name, a.shape, mybir.dt.from_np(a.dtype), kind="ExternalInput").ap())
    out = nc.dram_tensor("out", arrays["L0_attn_x"].shape, F32, kind="ExternalOutput").ap()
    sandwich_kernel(nc, *args, out)
    r = run_bass_kernel_spmd(nc, [arrays], core_ids=[0])
    return r.results[0]["out"]
```
